# Optimizing a Trainium2 kernel written in Bass

```python
import numpy as np
import jax
import jax.numpy as jnp

def _softmax(x, axis=-1):
    return jax.nn.softmax(x, axis=axis)

def _gelu(x):
    return jax.nn.gelu(x, approximate=True)

def _silu(x):
    return jax.nn.silu(x)

def _sigmoid(x):
    return jax.nn.sigmoid(x)

def _layernorm(x, axis=-1, eps=1e-05):
    m = jnp.mean(x, axis=axis, keepdims=True)
    v = jnp.var(x, axis=axis, keepdims=True)
    return (x - m) / jnp.sqrt(v + eps)

def _scatter_add(tgt, idx, src, axis=0):
    return tgt.at[idx].add(src)

def _segment_sum(src, seg, n):
    return jax.ops.segment_sum(src, seg, n)
kernel_name = 'mk_adaln_ffn_d1_seqx_r2_5ca7ce'

def setup_inputs(seed: int=0):
    np.random.seed(seed)
    _w = jnp.asarray

    def _rec_inputs():
        import jax
        import jax.numpy as jnp
        _rk = jax.random.key(seed)
        x = -7.109e-05 + 0.9999 * jax.random.normal(jax.random.fold_in(_rk, 1), (32, 128, 2048), jnp.float32)
        _lenS = 128 - jax.random.randint(jax.random.fold_in(_rk, 7), (32,), 0, max(1, 128 // 4) + 1, jnp.int32)
        _lenS2 = 128 - jax.random.randint(jax.random.fold_in(_rk, 8), (32,), 0, max(1, 128 // 4) + 1, jnp.int32)
        itok_B_0_30 = jax.random.randint(jax.random.fold_in(_rk, 11), (32,), 0, 31, jnp.int32)
        return (x, itok_B_0_30)
    x, itok_B_0_30 = _rec_inputs()

    def _L0_cond_setup():
        import jax, jax.numpy as jnp
        import numpy as np
        B, C, D, T, S = (64, 128, 128, 2048, 32)
        key = jax.random.key(seed)
        k1, k2, k3 = jax.random.split(key, 3)
        x = jax.random.normal(k1, (B, C, T), dtype=jnp.float32)
        subjects = jax.random.randint(k2, (B,), 0, S, dtype=jnp.int64)
        weights = jax.random.normal(k3, (S, C, D), dtype=jnp.float32) * (1.0 / np.sqrt(C))
        return {'x': x, 'subjects': subjects, 'weights': weights}
    _L0_cond_all = _L0_cond_setup()
    _L0_cond_in = {k: v for k, v in _L0_cond_all.items() if k in ('weights',)}
    del _L0_cond_all

    def _L0_ffn_setup():
        import jax, jax.numpy as jnp
        import numpy as np
        BATCH, TOK, DIM, OUT = (4, 1024, 2048, 2048)
        E, R, TOP_K = (8, 16, 2)
        SCALING = 16.0 / R
        key = jax.random.key(seed)
        ks = jax.random.split(key, 6)
        return {'x': jax.random.normal(ks[0], (BATCH, TOK, DIM), dtype=jnp.float32), 'W_base': jax.random.normal(ks[1], (OUT, DIM), dtype=jnp.float32) / np.sqrt(DIM), 'b_base': jax.random.normal(ks[2], (OUT,), dtype=jnp.float32) * 0.01, 'W_gate': jax.random.normal(ks[3], (E, DIM), dtype=jnp.float32) * 0.01, 'A': jax.random.normal(ks[4], (E, R, DIM), dtype=jnp.float32) / np.sqrt(DIM), 'B': jax.random.normal(ks[5], (OUT, OUT // OUT * R * 0 + R), dtype=jnp.float32)[None].repeat(E, 0) * 0.0 + jax.random.normal(ks[5], (E, OUT, R), dtype=jnp.float32) * 0.02}
    _L0_ffn_all = _L0_ffn_setup()
    _L0_ffn_in = {k: v for k, v in _L0_ffn_all.items() if k in ('W_base', 'b_base', 'W_gate', 'A', 'B')}
    del _L0_ffn_all
    return {'x': x, 'itok_B_0_30': itok_B_0_30, 'L0_cond_weights': _L0_cond_in['weights'], 'L0_ffn_W_base': _L0_ffn_in['W_base'], 'L0_ffn_b_base': _L0_ffn_in['b_base'], 'L0_ffn_W_gate': _L0_ffn_in['W_gate'], 'L0_ffn_A': _L0_ffn_in['A'], 'L0_ffn_B': _L0_ffn_in['B']}

def reference(x, itok_B_0_30, L0_cond_weights, L0_ffn_W_base, L0_ffn_b_base, L0_ffn_W_gate, L0_ffn_A, L0_ffn_B):
    import jax
    import jax.numpy as jnp

    def _L0_cond_ref(x, subjects, weights):
        import jax, jax.numpy as jnp
        import numpy as np
        B, C, D, T, S = (64, 128, 128, 2048, 32)
        w = weights[subjects]
        return jnp.einsum('bct,bcd->bdt', x, w)

    def _L0_ffn_ref(x, W_base, b_base, W_gate, A, B):
        import jax, jax.numpy as jnp
        import numpy as np
        BATCH, TOK, DIM, OUT = (4, 1024, 2048, 2048)
        E, R, TOP_K = (8, 16, 2)
        SCALING = 16.0 / R
        result = jnp.einsum('bnd,od->bno', x, W_base) + b_base
        logits = jnp.einsum('bnd,ed->bne', x, W_gate)
        probs = jax.nn.softmax(logits.astype(jnp.float32), axis=-1)
        top_p, top_i = jax.lax.top_k(probs, TOP_K)
        top_p = top_p / jnp.sum(top_p, axis=-1, keepdims=True)
        top_p = top_p.astype(x.dtype)
        route_w = jnp.sum(jax.nn.one_hot(top_i, E, dtype=x.dtype) * top_p[..., None], axis=-2)
        h = jnp.einsum('bnd,erd->bner', x, A)
        hw = h * route_w[..., None]
        delta = jnp.einsum('bner,eor->bno', hw, B)
        return result + delta * SCALING
    x = x + _L0_ffn_ref(_L0_cond_ref(x, itok_B_0_30, L0_cond_weights), L0_ffn_W_base, L0_ffn_b_base, L0_ffn_W_gate, L0_ffn_A, L0_ffn_B)
    return x

_drawn_inputs = setup_inputs


def setup_inputs(seed=0):
    import zlib

    import numpy as np

    out = dict(_drawn_inputs(seed))
    spreads = {}
    factors = {'L0_ffn_b_base': 8.0}
    for name, (base, spread) in spreads.items():
        noise = np.random.default_rng([zlib.crc32(name.encode()), seed]).standard_normal(out[name].shape)
        drawn = base * np.exp(spread * noise) if base else spread * noise
        out[name] = jnp.asarray(drawn.astype(out[name].dtype))
    for name, factor in factors.items():
        out[name] = (out[name] * factor).astype(out[name].dtype)
    return out
```

```python
from contextlib import ExitStack

import concourse.bass as bass
from concourse import mybir

P = 128
NB = 32
T = 2048
O = 2048
KC = T // P
OC = 512
NOC = O // OC
E, R = 8, 16
ER = E * R
HW = ER + E
GK = OC // P
NG = KC // GK
NW = O // P
SCALING = 16.0 / R

TOP = 2.0 ** 14
EXP_MASK = 0x7F800000
TINY = 2.0 ** -60
Y_DOWN = 2.0 ** -22
Y_UNIT = 2.0 ** -6

ALU = mybir.AluOpType
ACT = mybir.ActivationFunctionType
F32 = mybir.dt.float32
BF16 = mybir.dt.bfloat16
F16 = mybir.dt.float16
U32 = mybir.dt.uint32
I32 = mybir.dt.int32
AX_X = mybir.AxisListType.X
RMAX = bass.bass_isa.ReduceOp.max

GROUP_A = NG
GROUP_B = 2 * NG
GROUP_W = 3 * NG
HI_W = 2 * NG
FILL_A, FILL_G, FILL_GT, FILL_B, FILL_W = range(5)
ROWS_A, ROWS_G, ROWS_B, ROWS_W = range(4)


def group_y(b):
    return b * NG + (GROUP_W + NG * NW - NG)


def hi_y(b):
    return b * NG + (HI_W + NG * NW - NG)


def adaln_ffn_kernel(nc, x, idx, w_cond, w_base, b_base, w_gate, a_lora, b_lora, out):
    with ExitStack() as ctx:
        def sb(name, shape, dt=F32):
            return ctx.enter_context(nc.sbuf_tensor(name, shape, dt))

        def bank(name):
            return ctx.enter_context(nc.psum_tensor(name, [P, OC], F32))

        def sem(name):
            return ctx.enter_context(nc.semaphore(name))

        WT = sb("WT", [P, 2, KC, O], F16)
        AT = sb("AT", [P, 2, KC, HW], F16)
        BT = sb("BT", [P, 2, O], F16)
        inv_w = sb("inv_w", [P, O], BF16)
        inv_ag = sb("inv_ag", [P, HW])
        inv_b = sb("inv_b", [P, ER])
        bias = sb("bias", [P, O])
        X = [sb("x_even", [P, T]), sb("x_odd", [P, T])]
        XP = sb("x_parts", [P, 2, T], F16)
        Y = sb("y_parts", [P, 2, KC, P], F16)
        WC = sb("w_cond", [P, P])
        WCP = sb("w_cond_parts", [P, 2, P], F16)
        spare = sb("spare", [P, T])
        scaled_acc = sb("scaled_acc", [P, OC])
        h = sb("h", [P, HW])
        hw = sb("hw", [P, E, R])
        hwT = sb("hwT", [P, 2, P], F16)
        diag = sb("diag", [P, 2, P])
        ident = sb("ident", [P, P])
        ones = sb("ones", [P, P])
        iota_m8 = sb("iota_m8", [P, E])
        idx_sb = sb("idx", [1, NB], I32)
        amax = sb("amax", [P, 2])
        wait_taker = sb("wait_taker", [P, 2])
        amax_all = sb("amax_all", [P, 2])
        clamped = sb("clamped", [P, 2])
        pow2 = sb("pow2", [P, 2])
        rpow2 = sb("rpow2", [P, 2])
        xw_scale = sb("xw_scale", [P, 2])
        y_inv = sb("y_inv", [P, 2])
        row_max = sb("row_max", [P, 1])
        row_clamped = sb("row_clamped", [P, 1])
        row_pow2 = sb("row_pow2", [P, 1])
        row_rpow2 = sb("row_rpow2", [P, 1])
        row_scale = sb("row_scale", [P, 2])
        neg_max = sb("neg_max", [P, 1])
        shifted = sb("shifted", [P, E])
        exps = sb("exps", [P, E])
        exp_sum = sb("exp_sum", [P, 1])
        found = sb("found", [P, E])
        first = sb("first", [P, 1])
        pick1 = sb("pick1", [P, E])
        rest = sb("rest", [P, E])
        rest_max = sb("rest_max", [P, 1])
        pick2 = sb("pick2", [P, E])
        picked = sb("picked", [P, E])
        top_p = sb("top_p", [P, E])
        top_sum = sb("top_sum", [P, 1])
        rtop = sb("rtop", [P, 1])
        route = sb("route", [P, E])
        hw_max = sb("hw_max", [P, 1])
        hw_clamped = sb("hw_clamped", [P, 1])
        hw_pow2 = sb("hw_pow2", [P, 1])
        hw_rpow2 = sb("hw_rpow2", [P, 1])
        hw_scale = sb("hw_scale", [P, 1])
        hw_inv = sb("hw_inv", [P, 1])

        acc = [bank("acc0"), bank("acc1")]
        delta = [bank("delta0"), bank("delta1")]
        tr = [bank("tr0"), bank("tr1")]
        h_ps = bank("h_ps")
        small = bank("small")

        xp_f32 = XP[:, :, :].rearrange("p s t -> p (s t)").bitcast(F32)
        stage = [X[1][:, :], bias[:, :], spare[:, :], xp_f32]
        STAGE_A, STAGE_G, STAGE_B, STAGE_BJ = range(4)
        STAGE_BT = STAGE_B

        idx_in = sem("idx_in")
        x_in = [sem("x_even_in"), sem("x_odd_in")]
        w_in = sem("w_in")
        stage_in = [sem(f"stage{i}_in") for i in range(4)]
        bias_in = sem("bias_in")
        out_done = [sem("out_even_done"), sem("out_odd_done")]
        consts = sem("consts")
        pool_chain = sem("pool_chain")
        amax_ready = sem("amax_ready")
        amax_shared = sem("amax_shared")
        xw_scale_ready = sem("xw_scale_ready")
        xw_hi = sem("xw_hi")
        xw_parts = sem("xw_parts")
        bias_added = sem("bias_added")
        rows_scale = sem("rows_scale")
        rows_scaled = sem("rows_scaled")
        tr_filled = sem("tr_filled")
        tr_hi = sem("tr_hi")
        tr_emptied = sem("tr_emptied")
        small_filled = sem("small_filled")
        small_hi = sem("small_hi")
        small_emptied = sem("small_emptied")
        b_reordered = sem("b_reordered")
        bt_hi = sem("bt_hi")
        bt_parts = sem("bt_parts")
        h_ready = sem("h_ready")
        shifted_ready = sem("shifted_ready")
        exps_ready = sem("exps_ready")
        hw_ready = sem("hw_ready")
        hwT_filled = sem("hwT_filled")
        hwT_hi = sem("hwT_hi")
        hwT_ready = sem("hwT_ready")
        acc_done = sem("acc_done")
        acc_read = sem("acc_read")
        finished = sem("finished")
        dve_chain = sem("dve_chain")

        rows_w = w_base.rearrange("(n p) t -> n p t", p=P)
        a_rows = a_lora.rearrange("e r t -> (e r) t")
        b_rows = b_lora.rearrange("e (p j) r -> p e (j r)", p=P)
        bias_row = b_base.rearrange("(a o) -> a o", a=1).to_broadcast([P, O])
        NJ = O // P
        b_staged = stage[STAGE_B].rearrange("p (e j r) -> p e j r", e=E, j=NJ)
        b_columns = stage[STAGE_BJ].rearrange("p (j e r) -> p e j r", e=E, j=NJ)

        block = ctx.enter_context(nc.Block())

        @block.sync
        def _(sp):
            def load_xw(b, par):
                sp.dma_start(X[par][:, :], x[bass.ds(b, 1)].rearrange("a p t -> p (a t)")).then_inc(x_in[par], 16)
                row = sp.value_load(idx_sb[0:1, bass.ds(b, 1)], min_val=0, max_val=w_cond.shape[0] - 1)
                if not (isinstance(b, int) and b == 0):
                    sp.wait_ge(xw_parts, b)
                sp.dma_start(WC[:, :], w_cond[bass.ds(row, 1)].rearrange("a c d -> c (a d)")).then_inc(w_in, 16)

            def store(b, par):
                for oc in range(NOC):
                    sp.wait_ge(finished, b * NOC + (oc + 1))
                    sp.dma_start(out[bass.ds(b, 1), :, oc * OC:(oc + 1) * OC].rearrange("a p t -> p (a t)"),
                                 X[par][:, oc * OC:(oc + 1) * OC]).then_inc(out_done[par], 16)

            sp.dma_start(idx_sb[:, :], idx.rearrange("(a b) -> a b", a=1)).then_inc(idx_in, 16)
            sp.wait_ge(idx_in, 16)
            load_xw(0, 0)
            sp.dma_start(stage[STAGE_A], a_rows).then_inc(stage_in[STAGE_A], 16)
            sp.dma_start(stage[STAGE_G][0:E, :], w_gate).then_inc(stage_in[STAGE_G], 16)
            sp.dma_start(stage[STAGE_B].rearrange("p (e n) -> p e n", e=E), b_rows).then_inc(stage_in[STAGE_B], 16)
            for r in range(4):
                if r == 0:
                    sp.wait_ge(tr_filled, GROUP_A + NG)
                elif r == 1:
                    sp.wait_ge(small_filled, FILL_GT + 1)
                elif r == 2:
                    sp.wait_ge(bt_parts, 1)
                else:
                    sp.wait_ge(tr_filled, GROUP_B + NG)
                sp.dma_start(stage[r], rows_w[r]).then_inc(stage_in[r], 16)
            with sp.Fori(1, NW // 4) as q:
                for s in range(4):
                    sp.wait_ge(tr_filled, q * (4 * NG) + (GROUP_W + NG * (s - 3)))
                    sp.dma_start(stage[s], rows_w[bass.ds(q * 4 + s, 1)].rearrange("a p t -> p (a t)")
                                 ).then_inc(stage_in[s], 16)
            sp.wait_ge(tr_filled, GROUP_W + NG * (NW - 3))
            load_xw(1, 1)
            sp.wait_ge(tr_filled, GROUP_W + NG * (NW - 2))
            sp.dma_start(bias[:, :], bias_row).then_inc(bias_in, 16)

            sp.wait_ge(bias_added, 1)
            store(0, 0)
            sp.wait_ge(out_done[0], 16 * NOC)
            load_xw(2, 0)
            with sp.Fori(0, (NB - 4) // 2) as i:
                for b, par, n in ((i * 2 + 1, 1, i), (i * 2 + 2, 0, i + 1)):
                    store(b, par)
                    sp.wait_ge(out_done[par], (n + 1) * (16 * NOC))
                    load_xw(b + 2, par)
            store(NB - 3, 1)
            sp.wait_ge(out_done[1], 16 * NOC * (NB // 2 - 1))
            load_xw(NB - 1, 1)
            store(NB - 2, 0)
            store(NB - 1, 1)
            for par in range(2):
                sp.wait_ge(out_done[par], 16 * NOC * NB // 2)

        @block.gpsimd
        def _(pool):
            nc.gpsimd.memset(ident[:, :], 0.0).then_inc(pool_chain, 1)
            pool.wait_ge(pool_chain, 1)
            nc.gpsimd.affine_select(out=ident[:, :], in_=ident[:, :], compare_op=ALU.not_equal, fill=1.0, base=0,
                                    pattern=[[-1, P]], channel_multiplier=1).then_inc(consts, 1)
            for e in range(E):
                nc.gpsimd.memset(iota_m8[:, e:e + 1], float(e - E)).then_inc(consts, 1)
            nc.gpsimd.memset(ones[:, :], 1.0).then_inc(consts, 1)

            def share_maxima(b):
                pool.wait_ge(amax_ready, b + 1)
                nc.gpsimd.tensor_tensor(wait_taker[:, :], amax[:, :], ones[:, 0:2], ALU.mult)
                nc.gpsimd.partition_all_reduce(amax_all[:, :], amax[:, :], P, RMAX).then_inc(amax_shared, 1)

            def add_bias(par):
                nc.gpsimd.tensor_tensor(X[par][:, :], X[par][:, :], bias[:, :], ALU.add).then_inc(bias_added, 1)

            pool.wait_ge(consts, E + 2)
            share_maxima(0)
            pool.wait_ge(stage_in[STAGE_B], 16)
            pool.wait_ge(tr_filled, NG)
            nc.gpsimd.tensor_copy(b_columns, b_staged).then_inc(b_reordered, 1)
            share_maxima(1)
            pool.wait_ge(bias_in, 16)
            pool.wait_ge(finished, NOC)
            add_bias(0)
            pool.wait_ge(xw_parts, 2)
            add_bias(1)
            with pool.Fori(0, (NB - 2) // 2) as i:
                for b, par in ((i * 2 + 2, 0), (i * 2 + 3, 1)):
                    share_maxima(b)
                    pool.wait_ge(xw_parts, b + 1)
                    add_bias(par)

        @block.scalar
        def _(act):
            def split_x_hi(b, par):
                act.wait_ge(xw_scale_ready, b + 1)
                nc.scalar.activation(XP[:, 0, :], X[par][:, :], ACT.Copy, scale=xw_scale[:, 0:1])
                nc.scalar.activation(WCP[:, 0, :], WC[:, :], ACT.Copy, scale=xw_scale[:, 1:2]).then_inc(xw_hi, 1)

            def split_y_hi(group, hi, j):
                act.wait_ge(tr_filled, group + j + 1)
                nc.scalar.activation(Y[:, 0, GK * j:GK * (j + 1), :],
                                     tr[j % 2][:, :].rearrange("p (k n) -> p k n", k=GK),
                                     ACT.Copy, scale=Y_DOWN).then_inc(tr_hi, 1)

            def scale_rows(n, rows):
                act.wait_ge(rows_scale, n + 1)
                nc.scalar.activation(rows, rows, ACT.Copy,
                                     scale=row_scale[0:rows.shape[0], 0:1]).then_inc(rows_scaled, 1)

            def copy_scales(fill, dst):
                act.wait_ge(small_filled, fill + 1)
                nc.scalar.copy(dst, small[:, 0:dst.shape[1]]).then_inc(small_emptied, 1)

            def split_w_hi(r, group):
                for j in range(NG):
                    act.wait_ge(tr_filled, group + j + 1)
                    nc.scalar.activation(WT[:, 0, GK * j:GK * (j + 1), bass.ds(r * P, P)],
                                         tr[j % 2][:, :].rearrange("p (k n) -> p k n", k=GK),
                                         ACT.Copy).then_inc(tr_hi, 1)

            def exp_row(b):
                act.wait_ge(shifted_ready, b + 1)
                nc.scalar.activation(exps[:, :], shifted[:, :], ACT.Exp, accum_out=exp_sum[:, :]).then_inc(exps_ready, 1)

            def split_hwT_hi(b):
                act.wait_ge(hwT_filled, b + 1)
                nc.scalar.activation(hwT[:, 0, :], small[:, 0:P], ACT.Copy).then_inc(hwT_hi, 1)

            split_x_hi(0, 0)
            scale_rows(ROWS_A, stage[STAGE_A])
            for j in range(NG):
                split_y_hi(0, 0, j)
            scale_rows(ROWS_G, stage[STAGE_G][0:E, :])
            copy_scales(FILL_A, inv_ag[:, 0:ER])
            for j in range(NG):
                act.wait_ge(tr_filled, GROUP_A + j + 1)
                nc.scalar.activation(AT[:, 0, GK * j:GK * (j + 1), 0:ER],
                                     tr[j % 2][:, :].rearrange("p (k n) -> p k n", k=GK), ACT.Copy).then_inc(tr_hi, 1)
            copy_scales(FILL_G, inv_ag[:, ER:HW])
            act.wait_ge(small_filled, FILL_GT + 1)
            nc.scalar.activation(AT[:, 0, :, ER:HW], small[:, 0:KC * E].rearrange("p (k e) -> p k e", k=KC),
                                 ACT.Copy).then_inc(small_hi, 1)
            act.wait_ge(rows_scale, ROWS_B + 1)
            nc.scalar.activation(BT[:, 0, :], stage[STAGE_BT], ACT.Copy, scale=row_scale[:, 0:1]).then_inc(bt_hi, 1)
            copy_scales(FILL_B, inv_b[:, :])
            exp_row(0)
            scale_rows(ROWS_W, stage[0])
            copy_scales(FILL_W, inv_w[:, 0:P])
            for r in range(1, 4):
                scale_rows(ROWS_W + r, stage[r])
                split_w_hi(r - 1, GROUP_W + NG * (r - 1))
                if r == 1:
                    split_hwT_hi(0)
                copy_scales(FILL_W + r, inv_w[:, r * P:(r + 1) * P])
            with act.Fori(1, NW // 4) as q:
                for s in range(4):
                    r = q * 4 + s
                    scale_rows(r + ROWS_W, stage[s])
                    split_w_hi(r - 1, r * NG + (GROUP_W - NG))
                    copy_scales(r + FILL_W, inv_w[:, bass.ds(r * P, P)])
            split_w_hi(NW - 1, GROUP_W + NG * (NW - 1))
            split_x_hi(1, 1)
            for j in range(NG):
                split_y_hi(group_y(1), hi_y(1), j)

            def period(b, par):
                exp_row(b)
                split_hwT_hi(b)
                split_x_hi(b + 1, 1 - par)
                for j in range(NG):
                    split_y_hi(group_y(b + 1), hi_y(b + 1), j)

            with act.Fori(0, (NB - 2) // 2) as i:
                period(i * 2 + 1, 1)
                period(i * 2 + 2, 0)
            exp_row(NB - 1)
            split_hwT_hi(NB - 1)

        @block.vector
        def _(dve):
            chain = {"base": 0, "n": 0}

            def link(ins):
                chain["n"] += 1
                ins.then_inc(dve_chain, 1)
                dve.wait_ge(dve_chain, chain["base"] + chain["n"])

            def power_of_two(dst, top, src, mask_in):
                link(nc.vector.tensor_scalar(mask_in, src, TINY, None, ALU.max))
                link(nc.vector.tensor_scalar(dst.bitcast(U32), mask_in.bitcast(U32), EXP_MASK, None, ALU.bitwise_and))

            def find_x_maxima(b, par, n):
                dve.wait_ge(x_in[par], 16 * (n + 1))
                nc.vector.tensor_reduce(amax[:, 0:1], X[par][:, :], AX_X, ALU.max, apply_absolute_value=True)
                dve.wait_ge(w_in, 16 * (b + 1))
                nc.vector.tensor_reduce(amax[:, 1:2], WC[:, :], AX_X, ALU.max,
                                        apply_absolute_value=True).then_inc(amax_ready, 1)

            def scale_x(b, par):
                dve.wait_ge(amax_shared, b + 1)
                power_of_two(pow2[:, :], TOP, amax_all[:, :], clamped[:, :])
                link(nc.vector.reciprocal(rpow2[:, :], pow2[:, :]))
                nc.vector.tensor_scalar(xw_scale[:, :], rpow2[:, :], TOP, None, ALU.mult).then_inc(xw_scale_ready, 1)
                link(nc.vector.scalar_tensor_tensor(out=y_inv[:, par:par + 1], in0=pow2[:, 0:1], scalar=Y_UNIT,
                                                    in1=pow2[:, 1:2], op0=ALU.mult, op1=ALU.mult))

            def split_x_lo(b, par):
                dve.wait_ge(xw_hi, b + 1)
                nc.vector.scalar_tensor_tensor(out=XP[:, 1, :], in0=X[par][:, :], scalar=xw_scale[:, 0:1],
                                               in1=XP[:, 0, :], op0=ALU.mult, op1=ALU.subtract)
                nc.vector.scalar_tensor_tensor(out=WCP[:, 1, :], in0=WC[:, :], scalar=xw_scale[:, 1:2],
                                               in1=WCP[:, 0, :], op0=ALU.mult, op1=ALU.subtract).then_inc(xw_parts, 1)

            def split_lo(hi, dst, dst_hi, src, down=1.0):
                dve.wait_ge(tr_hi, hi + 1)
                nc.vector.scalar_tensor_tensor(out=dst, in0=src, scalar=down, in1=dst_hi,
                                               op0=ALU.mult, op1=ALU.subtract).then_inc(tr_emptied, 1)

            def bank_chunks(j):
                return tr[j % 2][:, :].rearrange("p (k n) -> p k n", k=GK)

            def split_y_lo(hi, j):
                ks = slice(GK * j, GK * (j + 1))
                split_lo(hi + j, Y[:, 1, ks, :], Y[:, 0, ks, :], bank_chunks(j), Y_DOWN)

            def split_w_lo(r, hi):
                for j in range(NG):
                    ks = slice(GK * j, GK * (j + 1))
                    split_lo(hi + j, WT[:, 1, ks, bass.ds(r * P, P)], WT[:, 0, ks, bass.ds(r * P, P)], bank_chunks(j))

            def scale_of_rows(rows, parity, diag_used, scaled):
                p = rows.shape[0]
                link(nc.vector.tensor_reduce(row_max[0:p, :], rows, AX_X, ALU.max, apply_absolute_value=True))
                power_of_two(row_pow2[0:p, :], TOP, row_max[0:p, :], row_clamped[0:p, :])
                link(nc.vector.reciprocal(row_rpow2[0:p, :], row_pow2[0:p, :]))
                if diag_used is not None:
                    dve.wait_ge(small_filled, diag_used)
                nc.vector.tensor_scalar(diag[0:p, parity, :], ident[0:p, :], row_pow2[0:p, :], 1.0 / TOP,
                                        ALU.mult, ALU.mult)
                if scaled is not None:
                    dve.wait_ge(rows_scaled, scaled)
                nc.vector.tensor_scalar(row_scale[0:p, 0:1], row_rpow2[0:p, :], TOP, None,
                                        ALU.mult).then_inc(rows_scale, 1)

            def routing(b, par):
                dve.wait_ge(h_ready, b + 1)
                link(nc.vector.scalar_tensor_tensor(out=h[:, :], in0=h_ps[:, 0:HW], scalar=y_inv[:, par:par + 1],
                                                    in1=inv_ag[:, :], op0=ALU.mult, op1=ALU.mult))
                link(nc.vector.tensor_reduce(neg_max[:, :], h[:, ER:HW], AX_X, ALU.max, negate=True))
                nc.vector.tensor_scalar(shifted[:, :], h[:, ER:HW], neg_max[:, :], None,
                                        ALU.add).then_inc(shifted_ready, 1)
                dve.wait_ge(shifted_ready, b + 1)
                link(nc.vector.scalar_tensor_tensor(out=found[:, :], in0=shifted[:, :], scalar=0.0, in1=iota_m8[:, :],
                                                    op0=ALU.is_equal, op1=ALU.mult))
                link(nc.vector.tensor_reduce(first[:, :], found[:, :], AX_X, ALU.min))
                link(nc.vector.tensor_scalar(pick1[:, :], iota_m8[:, :], first[:, :], None, ALU.is_equal))
                link(nc.vector.scalar_tensor_tensor(out=rest[:, :], in0=pick1[:, :], scalar=-1e38, in1=shifted[:, :],
                                                    op0=ALU.mult, op1=ALU.add))
                link(nc.vector.tensor_reduce(rest_max[:, :], rest[:, :], AX_X, ALU.max))
                link(nc.vector.scalar_tensor_tensor(out=found[:, :], in0=rest[:, :], scalar=rest_max[:, :],
                                                    in1=iota_m8[:, :], op0=ALU.is_equal, op1=ALU.mult))
                link(nc.vector.tensor_reduce(first[:, :], found[:, :], AX_X, ALU.min))
                link(nc.vector.tensor_scalar(pick2[:, :], iota_m8[:, :], first[:, :], None, ALU.is_equal))
                link(nc.vector.tensor_tensor(picked[:, :], pick1[:, :], pick2[:, :], ALU.add))
                dve.wait_ge(exps_ready, b + 1)
                link(nc.vector.reciprocal(rtop[:, :], exp_sum[:, :]))
                link(nc.vector.scalar_tensor_tensor(out=top_p[:, :], in0=exps[:, :], scalar=rtop[:, :],
                                                    in1=picked[:, :], op0=ALU.mult, op1=ALU.mult))
                link(nc.vector.tensor_reduce(top_sum[:, :], top_p[:, :], AX_X, ALU.add))
                link(nc.vector.reciprocal(rtop[:, :], top_sum[:, :]))
                link(nc.vector.tensor_scalar(route[:, :], top_p[:, :], rtop[:, :], SCALING, ALU.mult, ALU.mult))
                link(nc.vector.tensor_tensor(hw[:, :, :], h[:, 0:ER].rearrange("p (e r) -> p e r", e=E),
                                             route[:, :].rearrange("p (e a) -> p e a", a=1).to_broadcast([P, E, R]),
                                             ALU.mult))
                hw_flat = hw[:, :, :].rearrange("p e r -> p (e r)")
                link(nc.vector.tensor_tensor(hw_flat, hw_flat, inv_b[:, :], ALU.mult))
                link(nc.vector.tensor_reduce(hw_max[:, :], hw_flat, AX_X, ALU.max, apply_absolute_value=True))
                power_of_two(hw_pow2[:, :], TOP, hw_max[:, :], hw_clamped[:, :])
                link(nc.vector.reciprocal(hw_rpow2[:, :], hw_pow2[:, :]))
                nc.vector.tensor_scalar(hw_inv[:, :], hw_pow2[:, :], 1.0 / TOP, None, ALU.mult)
                nc.vector.tensor_scalar(hw_flat, hw_flat, hw_rpow2[:, :], TOP, ALU.mult, ALU.mult).then_inc(hw_ready, 1)

            def split_hwT_lo(b):
                dve.wait_ge(hwT_hi, b + 1)
                nc.vector.scalar_tensor_tensor(out=hwT[:, 1, :], in0=small[:, 0:P], scalar=1.0, in1=hwT[:, 0, :],
                                               op0=ALU.mult, op1=ALU.subtract).then_inc(hwT_ready, 1)

            def finish(b, par, oc, half):
                cols = bass.ds(oc * OC, OC)
                if not (isinstance(b, int) and b == 0):
                    dve.wait_ge(finished, b * NOC + oc)
                dve.wait_ge(acc_done, b * NOC + oc + 1)
                nc.vector.scalar_tensor_tensor(out=scaled_acc[:, :], in0=acc[half][:, :], scalar=y_inv[:, par:par + 1],
                                               in1=inv_w[:, cols], op0=ALU.mult, op1=ALU.mult)
                nc.vector.scalar_tensor_tensor(out=X[par][:, cols], in0=delta[half][:, :], scalar=hw_inv[:, :],
                                               in1=X[par][:, cols], op0=ALU.mult, op1=ALU.add).then_inc(acc_read, 1)
                dve.wait_ge(acc_read, b * NOC + oc + 1)
                nc.vector.tensor_tensor(X[par][:, cols], X[par][:, cols], scaled_acc[:, :], ALU.add).then_inc(finished, 1)

            find_x_maxima(0, 0, 0)
            dve.wait_ge(consts, E + 2)
            dve.wait_ge(stage_in[STAGE_A], 16)
            scale_of_rows(stage[STAGE_A], ROWS_A % 2, None, None)
            scale_x(0, 0)
            split_x_lo(0, 0)
            dve.wait_ge(stage_in[STAGE_G], 16)
            scale_of_rows(stage[STAGE_G][0:E, :], ROWS_G % 2, None, 1)
            for j in range(NG):
                split_y_lo(0, j)
            for j in range(NG):
                ks = slice(GK * j, GK * (j + 1))
                split_lo(NG + j, AT[:, 1, ks, 0:ER], AT[:, 0, ks, 0:ER], bank_chunks(j))
            dve.wait_ge(small_hi, 1)
            nc.vector.scalar_tensor_tensor(out=AT[:, 1, :, ER:HW],
                                           in0=small[:, 0:KC * E].rearrange("p (k e) -> p k e", k=KC), scalar=1.0,
                                           in1=AT[:, 0, :, ER:HW], op0=ALU.mult,
                                           op1=ALU.subtract).then_inc(small_emptied, 1)
            bt_cols = stage[STAGE_BT].rearrange("q (p j) -> q j p", j=NJ)
            for j in range(NG):
                dve.wait_ge(tr_filled, GROUP_B + j + 1)
                nc.vector.tensor_copy(bt_cols[:, GK * j:GK * (j + 1), :], bank_chunks(j)).then_inc(tr_emptied, 1)
            dve.wait_ge(tr_emptied, GROUP_B + NG)
            scale_of_rows(stage[STAGE_BT], ROWS_B % 2, FILL_A + 1, 2)
            dve.wait_ge(bt_hi, 1)
            nc.vector.scalar_tensor_tensor(out=BT[:, 1, :], in0=stage[STAGE_BT], scalar=row_scale[:, 0:1],
                                           in1=BT[:, 0, :], op0=ALU.mult, op1=ALU.subtract).then_inc(bt_parts, 1)
            dve.wait_ge(small_emptied, FILL_B + 1)
            routing(0, 0)
            for r in range(4):
                dve.wait_ge(stage_in[r], 16 * (2 if r < 3 else 1))
                scale_of_rows(stage[r], (ROWS_W + r) % 2, [FILL_G + 1, FILL_B + 1, FILL_W + 1, FILL_W + 2][r], 2 + r)
                if r > 0:
                    split_w_lo(r - 1, HI_W + NG * (r - 1))
                if r == 1:
                    split_hwT_lo(0)

            def w_blocks(q):
                for s in range(4):
                    r = q * 4 + s
                    dve.wait_ge(stage_in[s], (q + (2 if s < 3 else 1)) * 16)
                    scale_of_rows(stage[s], (ROWS_W + s) % 2, r + (FILL_W - 1), r + 2)
                    split_w_lo(r - 1, r * NG + (HI_W - NG))
                dve.wait_ge(small_emptied, q * 4 + FILL_W)
                finish(0, 0, q - 1, 0)

            start, per_block = chain["n"], 4
            with dve.Fori(1, NW // 4) as q:
                chain["base"], chain["n"] = q * (4 * per_block) + (start - 4 * per_block), 0
                w_blocks(q)
                assert chain["n"] == 4 * per_block
            chain["base"], chain["n"] = start + (NW - 4) * per_block, 0
            split_w_lo(NW - 1, HI_W + NG * (NW - 1))
            dve.wait_ge(small_emptied, FILL_W + NW)
            find_x_maxima(1, 1, 0)
            scale_x(1, 1)
            split_x_lo(1, 1)
            for j in range(NG):
                split_y_lo(hi_y(1), j)
            finish(0, 0, NOC - 1, 1)

            def period(b, par, n):
                routing(b, par)
                split_hwT_lo(b)
                find_x_maxima(b + 1, 1 - par, n)
                scale_x(b + 1, 1 - par)
                split_x_lo(b + 1, 1 - par)
                dve.wait_ge(bias_added, b + 1)
                for oc in range(NOC - 1):
                    finish(b, par, oc, oc % 2)
                for j in range(NG):
                    split_y_lo(hi_y(b + 1), j)
                finish(b, par, NOC - 1, (NOC - 1) % 2)

            start, per_row = chain["base"] + chain["n"], 26
            with dve.Fori(0, (NB - 2) // 2) as i:
                for k, (b, par, n) in enumerate(((i * 2 + 1, 1, i + 1), (i * 2 + 2, 0, i + 1))):
                    chain["base"], chain["n"] = i * (2 * per_row) + (start + k * per_row), 0
                    period(b, par, n)
                    assert chain["n"] == per_row, chain["n"]
            chain["base"], chain["n"] = start + (NB - 2) * per_row, 0
            routing(NB - 1, 1)
            split_hwT_lo(NB - 1)
            dve.wait_ge(bias_added, NB)
            for oc in range(NOC):
                finish(NB - 1, 1, oc, oc % 2)

        @block.tensor
        def _(pe):
            def three(dst, lhs, rhs, start, stop):
                nc.tensor.matmul(dst, lhs[0], rhs[0], start=start, stop=False)
                nc.tensor.matmul(dst, lhs[0], rhs[1], start=False, stop=False)
                return nc.tensor.matmul(dst, lhs[1], rhs[0], start=False, stop=stop)

            def cond_group(group, j):
                if not (isinstance(group, int) and group + j < 2):
                    pe.wait_ge(tr_emptied, group + j - 1)
                for c in range(GK):
                    ks = slice((GK * j + c) * P, (GK * j + c + 1) * P)
                    mm = three(tr[j % 2][:, c * P:(c + 1) * P], [XP[:, s, ks] for s in range(2)],
                               [WCP[:, s, :] for s in range(2)], True, True)
                mm.then_inc(tr_filled, 1)

            def lora_features(b, group):
                for j in range(NG):
                    pe.wait_ge(tr_emptied, group + j + 1)
                    for k in range(GK * j, GK * (j + 1)):
                        mm = three(h_ps[:, 0:HW], [Y[:, s, k, :] for s in range(2)], [AT[:, s, k, :] for s in range(2)],
                                   k == 0, k == KC - 1)
                mm.then_inc(h_ready, 1)

            def base_step(oc, half, k):
                cols = bass.ds(oc * OC, OC)
                three(acc[half][:, :], [Y[:, s, k, :] for s in range(2)], [WT[:, s, k, cols] for s in range(2)],
                      k == 0, k == KC - 1)

            def delta_step(oc, half):
                cols = bass.ds(oc * OC, OC)
                three(delta[half][:, :], [hwT[:, s, :] for s in range(2)], [BT[:, s, cols] for s in range(2)],
                      True, True).then_inc(acc_done, 1)

            def transpose_hw(b):
                pe.wait_ge(hw_ready, b + 1)
                nc.tensor.transpose(small[:, 0:P], hw[:, :, :].rearrange("p e r -> p (e r)"),
                                    ident[:, :]).then_inc(hwT_filled, 1)

            def spread_scales(parity, ready, emptied, p=P):
                pe.wait_ge(rows_scale, ready)
                if emptied is not None:
                    pe.wait_ge(small_emptied, emptied)
                nc.tensor.matmul(small[:, 0:p], ones[0:p, :], diag[0:p, parity, 0:p],
                                 start=True, stop=True).then_inc(small_filled, 1)

            def transpose_group(src, group, j):
                pe.wait_ge(tr_emptied, group + j - 1)
                for c in range(GK):
                    t = nc.tensor.transpose(tr[j % 2][:, c * P:(c + 1) * P], src(GK * j + c), ident[:, :])
                t.then_inc(tr_filled, 1)

            def chunk_of(rows):
                return lambda k: rows[:, k * P:(k + 1) * P]

            pe.wait_ge(xw_parts, 1)
            for j in range(NG):
                cond_group(0, j)
            pe.wait_ge(consts, E + 2)
            spread_scales(ROWS_A % 2, ROWS_A + 1, None)
            pe.wait_ge(rows_scaled, 1)
            for j in range(NG):
                transpose_group(chunk_of(stage[STAGE_A]), GROUP_A, j)
            spread_scales(ROWS_G % 2, ROWS_G + 1, FILL_A + 1, E)
            pe.wait_ge(rows_scaled, 2)
            pe.wait_ge(small_emptied, FILL_G + 1)
            for k in range(KC):
                t = nc.tensor.transpose(small[:, k * E:(k + 1) * E], stage[STAGE_G][0:E, k * P:(k + 1) * P],
                                        ident[0:E, 0:E])
            t.then_inc(small_filled, 1)
            pe.wait_ge(b_reordered, 1)
            for j in range(NG):
                transpose_group(chunk_of(stage[STAGE_BJ]), GROUP_B, j)
            pe.wait_ge(small_emptied, FILL_GT + 1)
            lora_features(0, 0)
            spread_scales(ROWS_B % 2, ROWS_B + 1, None)
            for r in range(4):
                spread_scales((ROWS_W + r) % 2, ROWS_W + r + 1, FILL_W + r)
                pe.wait_ge(rows_scaled, 3 + r)
                for j in range(NG):
                    transpose_group(chunk_of(stage[r]), GROUP_W + NG * r, j)
                if r == 0:
                    pe.wait_ge(small_emptied, FILL_W + 1)
                    transpose_hw(0)
                    pe.wait_ge(hwT_ready, 1)
            beside = {(s, j): [] for s in range(4) for j in range(NG)}
            for k, slot in zip(range(KC), [(0, 1), (0, 1), (0, 2), (0, 2), (0, 3), (0, 3), (1, 0), (1, 0), (1, 1),
                                           (1, 2), (1, 3), (2, 0), (2, 0), (2, 1), (2, 2), (2, 3)]):
                beside[slot].append(k)
            with pe.Fori(1, NW // 4) as q:
                for s in range(4):
                    spread_scales((ROWS_W + s) % 2, q * 4 + (ROWS_W + s + 1), q * 4 + (FILL_W + s))
                    pe.wait_ge(rows_scaled, q * 4 + (3 + s))
                    for j in range(NG):
                        transpose_group(chunk_of(stage[s]), q * (4 * NG) + (GROUP_W + NG * s), j)
                        for k in beside[s, j]:
                            base_step(q - 1, 0, k)
                    if s == 2:
                        delta_step(q - 1, 0)
            pe.wait_ge(tr_emptied, GROUP_W + NG * NW)
            pe.wait_ge(small_emptied, FILL_W + NW)
            for k in range(KC):
                base_step(NOC - 1, 1, k)
                if k in (9, 11, 13, 15):
                    if k == 9:
                        pe.wait_ge(xw_parts, 2)
                    cond_group(group_y(1), (k - 9) // 2)
            delta_step(NOC - 1, 1)

            def period(b, last=False):
                lora_features(b, group_y(b))
                for oc in range(NOC):
                    pe.wait_ge(acc_read, b * NOC + (oc - 1))
                    for k in range(KC):
                        base_step(oc, oc % 2, k)
                        if oc == 1 and k == GK - 1:
                            pe.wait_ge(hwT_ready, b + 1)
                            delta_step(0, 0)
                        if oc == NOC - 1 and k % GK == GK - 1 and not last:
                            if k == GK - 1:
                                pe.wait_ge(xw_parts, b + 2)
                            cond_group(group_y(b + 1), k // GK)
                    if oc == 0:
                        transpose_hw(b)
                    else:
                        delta_step(oc, oc % 2)

            with pe.Fori(1, NB - 1) as b:
                period(b)
            period(NB - 1, last=True)


_INS = ['x', 'itok_B_0_30', 'L0_cond_weights', 'L0_ffn_W_base', 'L0_ffn_b_base', 'L0_ffn_W_gate', 'L0_ffn_A',
        'L0_ffn_B']
_OUTS = [((NB, P, O), 'float32')]


def kernel(**inputs):
    import numpy as _np
    import concourse.bacc as _bacc
    from concourse import mybir as _mybir
    from concourse.bass_utils import run_bass_kernel_spmd as _run

    nc = _bacc.Bacc("TRN2", target_bir_lowering=False, num_devices=1)
    arrays, args = {}, []
    for name in _INS:
        a = _np.ascontiguousarray(inputs[name])
        arrays[f"in_{name}_dram"] = a
        args.append(nc.dram_tensor(f"in_{name}_dram", a.shape, _mybir.dt.from_np(a.dtype), kind="ExternalInput").ap())
    for i, (shape, dtype) in enumerate(_OUTS):
        dt = _mybir.dt.from_np(_np.dtype(dtype))
        args.append(nc.dram_tensor(f"out_{i}_dram", shape, dt, kind="ExternalOutput").ap())
    adaln_ffn_kernel(nc, *args)
    r = _run(nc, [arrays], core_ids=[0])
    got = tuple(r.results[0][f"out_{i}_dram"] for i in range(len(_OUTS)))
    return got[0]
```

```python
from contextlib import ExitStack

import concourse.bass as bass
from concourse import mybir

P = 128
NB = 32
T = 2048
O = 2048
KC = T // P
OC = 512
NOC = O // OC
E, R = 8, 16
ER = E * R
HW = ER + E
GK = OC // P
NG = KC // GK
NW = O // P
SCALING = 16.0 / R

TOP = 2.0 ** 14
EXP_MASK = 0x7F800000
TINY = 2.0 ** -60
Y_DOWN = 2.0 ** -22
Y_UNIT = 2.0 ** -6

ALU = mybir.AluOpType
ACT = mybir.ActivationFunctionType
F32 = mybir.dt.float32
BF16 = mybir.dt.bfloat16
F16 = mybir.dt.float16
U32 = mybir.dt.uint32
I32 = mybir.dt.int32
AX_X = mybir.AxisListType.X
RMAX = bass.bass_isa.ReduceOp.max

GROUP_A = NG
GROUP_B = 2 * NG
GROUP_W = 3 * NG
SPLIT_W = 2 * NG
FILL_A, FILL_G, FILL_GT, FILL_W, FILL_B = range(5)
ROWS_A, ROWS_G, ROWS_W, ROWS_B = range(4)


def group_y(b):
    return b * NG + (GROUP_W + NG * NW - NG)


def split_y(b):
    return b * NG + (SPLIT_W + NG * NW - NG)


def adaln_ffn_kernel(nc, x, idx, w_cond, w_base, b_base, w_gate, a_lora, b_lora, out):
    with ExitStack() as ctx:
        def sb(name, shape, dt=F32):
            return ctx.enter_context(nc.sbuf_tensor(name, shape, dt))

        def bank(name):
            return ctx.enter_context(nc.psum_tensor(name, [P, OC], F32))

        def sem(name):
            return ctx.enter_context(nc.semaphore(name))

        WT = sb("WT", [P, 2, KC, O], F16)
        AT = sb("AT", [P, 2, KC, HW], F16)
        BT = sb("BT", [P, 2, O], F16)
        inv_w = sb("inv_w", [P, O], BF16)
        inv_ag = sb("inv_ag", [P, HW])
        inv_b = sb("inv_b", [P, ER])
        bias = sb("bias", [P, O])
        X = [sb("x_even", [P, T]), sb("x_odd", [P, T])]
        XP = sb("x_parts", [P, 2, T], F16)
        Y = sb("y_parts", [P, 2, KC, P], F16)
        WC = sb("w_cond", [P, P])
        WCP = sb("w_cond_parts", [P, 2, P], F16)
        spare = sb("spare", [P, T])
        scaled_acc = sb("scaled_acc", [P, OC])
        h = sb("h", [P, HW])
        hw = sb("hw", [P, E, R])
        hwT = sb("hwT", [P, 2, P], F16)
        diag = sb("diag", [P, 2, 2, P])
        ident = sb("ident", [P, P])
        ones = sb("ones", [P, P])
        iota_m8 = sb("iota_m8", [P, E])
        idx_sb = sb("idx", [1, NB], I32)
        amax = sb("amax", [P, 2])
        wait_taker = sb("wait_taker", [P, 2])
        amax_all = sb("amax_all", [P, 2])
        clamped = sb("clamped", [P, 2])
        pow2 = sb("pow2", [P, 2])
        rpow2 = sb("rpow2", [P, 2])
        xw_scale = sb("xw_scale", [P, 2])
        y_inv = sb("y_inv", [P, 2])
        row_max = sb("row_max", [P, 1])
        row_clamped = sb("row_clamped", [P, 1])
        row_pow2 = sb("row_pow2", [P, 1])
        row_rpow2 = sb("row_rpow2", [P, 1])
        b_scale = sb("b_scale", [P, 1])
        neg_max = sb("neg_max", [P, 1])
        shifted = sb("shifted", [P, E])
        exps = sb("exps", [P, E])
        exp_sum = sb("exp_sum", [P, 1])
        found = sb("found", [P, E])
        first = sb("first", [P, 1])
        pick1 = sb("pick1", [P, E])
        rest = sb("rest", [P, E])
        rest_max = sb("rest_max", [P, 1])
        pick2 = sb("pick2", [P, E])
        picked = sb("picked", [P, E])
        top_p = sb("top_p", [P, E])
        top_sum = sb("top_sum", [P, 1])
        rtop = sb("rtop", [P, 1])
        route = sb("route", [P, E])
        hw_max = sb("hw_max", [P, 1])
        hw_clamped = sb("hw_clamped", [P, 1])
        hw_pow2 = sb("hw_pow2", [P, 1])
        hw_rpow2 = sb("hw_rpow2", [P, 1])
        hw_scale = sb("hw_scale", [P, 1])
        hw_inv = sb("hw_inv", [P, 1])

        acc = [bank("acc0"), bank("acc1")]
        delta = [bank("delta0"), bank("delta1")]
        tr = [bank("tr0"), bank("tr1")]
        ring = tr + [acc[1], delta[1]]
        h_ps = bank("h_ps")
        small = bank("small")

        xp_f32 = XP[:, :, :].rearrange("p s t -> p (s t)").bitcast(F32)
        stage = [X[1][:, :], bias[:, :], spare[:, :], xp_f32]
        STAGE_A, STAGE_G, STAGE_B, STAGE_BJ = range(4)
        STAGE_BT = STAGE_B

        idx_in = sem("idx_in")
        x_in = [sem("x_even_in"), sem("x_odd_in")]
        w_in = sem("w_in")
        stage_in = [sem(f"stage{i}_in") for i in range(4)]
        bias_in = sem("bias_in")
        out_done = [sem("out_even_done"), sem("out_odd_done")]
        consts = sem("consts")
        pool_chain = sem("pool_chain")
        amax_ready = sem("amax_ready")
        amax_shared = sem("amax_shared")
        xw_scale_ready = sem("xw_scale_ready")
        xw_hi = sem("xw_hi")
        xw_parts = sem("xw_parts")
        bias_added = sem("bias_added")
        rows_scale = sem("rows_scale")
        tr_filled = sem("tr_filled")
        tr_hi = sem("tr_hi")
        tr_emptied = sem("tr_emptied")
        small_filled = sem("small_filled")
        small_hi = sem("small_hi")
        small_emptied = sem("small_emptied")
        b_reordered = sem("b_reordered")
        bt_copied = sem("bt_copied")
        bt_hi = sem("bt_hi")
        bt_parts = sem("bt_parts")
        h_ready = sem("h_ready")
        shifted_ready = sem("shifted_ready")
        exps_ready = sem("exps_ready")
        hw_ready = sem("hw_ready")
        hwT_filled = sem("hwT_filled")
        hwT_hi = sem("hwT_hi")
        hwT_ready = sem("hwT_ready")
        acc_done = sem("acc_done")
        acc_read = sem("acc_read")
        finished = sem("finished")
        dve_chain = sem("dve_chain")

        rows_w = w_base.rearrange("(n p) t -> n p t", p=P)
        a_rows = a_lora.rearrange("e r t -> (e r) t")
        b_rows = b_lora.rearrange("e (p j) r -> p e (j r)", p=P)
        bias_row = b_base.rearrange("(a o) -> a o", a=1).to_broadcast([P, O])
        NJ = O // P
        b_staged = stage[STAGE_B].rearrange("p (e j r) -> p e j r", e=E, j=NJ)
        b_columns = stage[STAGE_BJ].rearrange("p (j e r) -> p e j r", e=E, j=NJ)

        def chunks(banks, j):
            return banks[j % len(banks)][:, :].rearrange("p (k n) -> p k n", k=GK)

        block = ctx.enter_context(nc.Block())

        @block.sync
        def _(sp):
            def load_xw(b, par):
                sp.dma_start(X[par][:, :], x[bass.ds(b, 1)].rearrange("a p t -> p (a t)")).then_inc(x_in[par], 16)
                row = sp.value_load(idx_sb[0:1, bass.ds(b, 1)], min_val=0, max_val=w_cond.shape[0] - 1)
                if not (isinstance(b, int) and b == 0):
                    sp.wait_ge(xw_parts, b)
                sp.dma_start(WC[:, :], w_cond[bass.ds(row, 1)].rearrange("a c d -> c (a d)")).then_inc(w_in, 16)

            def store(b, par):
                for oc in range(NOC):
                    sp.wait_ge(finished, b * NOC + (oc + 1))
                    sp.dma_start(out[bass.ds(b, 1), :, oc * OC:(oc + 1) * OC].rearrange("a p t -> p (a t)"),
                                 X[par][:, oc * OC:(oc + 1) * OC]).then_inc(out_done[par], 16)

            sp.dma_start(idx_sb[:, :], idx.rearrange("(a b) -> a b", a=1)).then_inc(idx_in, 16)
            sp.wait_ge(idx_in, 16)
            load_xw(0, 0)
            sp.dma_start(stage[STAGE_A], a_rows).then_inc(stage_in[STAGE_A], 16)
            sp.dma_start(stage[STAGE_G][0:E, :], w_gate).then_inc(stage_in[STAGE_G], 16)
            sp.dma_start(stage[STAGE_B].rearrange("p (e n) -> p e n", e=E), b_rows).then_inc(stage_in[STAGE_B], 16)
            for r in range(4):
                if r == 0:
                    sp.wait_ge(tr_filled, GROUP_A + NG)
                elif r == 1:
                    sp.wait_ge(small_filled, FILL_GT + 1)
                elif r == 2:
                    sp.wait_ge(bt_parts, 1)
                else:
                    sp.wait_ge(tr_filled, GROUP_B + NG)
                sp.dma_start(stage[r], rows_w[r]).then_inc(stage_in[r], 16)
            with sp.Fori(1, NW // 4) as q:
                for s in range(4):
                    sp.wait_ge(tr_filled, q * (4 * NG) + (GROUP_W + NG * (s - 3)))
                    sp.dma_start(stage[s], rows_w[bass.ds(q * 4 + s, 1)].rearrange("a p t -> p (a t)")
                                 ).then_inc(stage_in[s], 16)
            sp.wait_ge(tr_filled, GROUP_W + NG * (NW - 3))
            load_xw(1, 1)
            sp.wait_ge(tr_filled, GROUP_W + NG * (NW - 2))
            sp.dma_start(bias[:, :], bias_row).then_inc(bias_in, 16)

            sp.wait_ge(bias_added, 1)
            store(0, 0)
            sp.wait_ge(out_done[0], 16 * NOC)
            load_xw(2, 0)
            with sp.Fori(0, (NB - 4) // 2) as i:
                for b, par, n in ((i * 2 + 1, 1, i), (i * 2 + 2, 0, i + 1)):
                    store(b, par)
                    sp.wait_ge(out_done[par], (n + 1) * (16 * NOC))
                    load_xw(b + 2, par)
            store(NB - 3, 1)
            sp.wait_ge(out_done[1], 16 * NOC * (NB // 2 - 1))
            load_xw(NB - 1, 1)
            store(NB - 2, 0)
            store(NB - 1, 1)
            for par in range(2):
                sp.wait_ge(out_done[par], 16 * NOC * NB // 2)

        @block.gpsimd
        def _(pool):
            nc.gpsimd.memset(ident[:, :], 0.0).then_inc(pool_chain, 1)
            pool.wait_ge(pool_chain, 1)
            nc.gpsimd.affine_select(out=ident[:, :], in_=ident[:, :], compare_op=ALU.not_equal, fill=1.0, base=0,
                                    pattern=[[-1, P]], channel_multiplier=1).then_inc(consts, 1)
            for e in range(E):
                nc.gpsimd.memset(iota_m8[:, e:e + 1], float(e - E)).then_inc(consts, 1)
            nc.gpsimd.memset(ones[:, :], 1.0).then_inc(consts, 1)

            def share_maxima(b):
                pool.wait_ge(amax_ready, b + 1)
                nc.gpsimd.tensor_tensor(wait_taker[:, :], amax[:, :], ones[:, 0:2], ALU.mult)
                nc.gpsimd.partition_all_reduce(amax_all[:, :], amax[:, :], P, RMAX).then_inc(amax_shared, 1)

            def add_bias(par):
                nc.gpsimd.tensor_tensor(X[par][:, :], X[par][:, :], bias[:, :], ALU.add).then_inc(bias_added, 1)

            pool.wait_ge(consts, E + 2)
            share_maxima(0)
            pool.wait_ge(stage_in[STAGE_B], 16)
            pool.wait_ge(tr_filled, NG)
            nc.gpsimd.tensor_copy(b_columns, b_staged).then_inc(b_reordered, 1)
            share_maxima(1)
            pool.wait_ge(bias_in, 16)
            pool.wait_ge(finished, NOC)
            add_bias(0)
            pool.wait_ge(xw_parts, 2)
            add_bias(1)
            with pool.Fori(0, (NB - 2) // 2) as i:
                for b, par in ((i * 2 + 2, 0), (i * 2 + 3, 1)):
                    share_maxima(b)
                    pool.wait_ge(xw_parts, b + 1)
                    add_bias(par)

        @block.scalar
        def _(act):
            def split_x_hi(b, par):
                act.wait_ge(xw_scale_ready, b + 1)
                nc.scalar.activation(XP[:, 0, :], X[par][:, :], ACT.Copy, scale=xw_scale[:, 0:1])
                nc.scalar.activation(WCP[:, 0, :], WC[:, :], ACT.Copy, scale=xw_scale[:, 1:2]).then_inc(xw_hi, 1)

            def split_y_hi(group, banks, j):
                act.wait_ge(tr_filled, group + j + 1)
                nc.scalar.activation(Y[:, 0, GK * j:GK * (j + 1), :], chunks(banks, j),
                                     ACT.Copy, scale=Y_DOWN).then_inc(tr_hi, 1)

            def copy_scales(fill, dst):
                act.wait_ge(small_filled, fill + 1)
                nc.scalar.copy(dst, small[:, 0:dst.shape[1]]).then_inc(small_emptied, 1)

            def split_w_hi(r, group):
                for j in range(NG):
                    act.wait_ge(tr_filled, group + j + 1)
                    nc.scalar.activation(WT[:, 0, GK * j:GK * (j + 1), bass.ds(r * P, P)],
                                         chunks(ring, j), ACT.Copy).then_inc(tr_hi, 1)

            def exp_row(b):
                act.wait_ge(shifted_ready, b + 1)
                nc.scalar.activation(exps[:, :], shifted[:, :], ACT.Exp, accum_out=exp_sum[:, :]).then_inc(exps_ready, 1)

            def split_hwT_hi(b):
                act.wait_ge(hwT_filled, b + 1)
                nc.scalar.activation(hwT[:, 0, :], small[:, 0:P], ACT.Copy).then_inc(hwT_hi, 1)

            split_x_hi(0, 0)
            for j in range(NG):
                split_y_hi(0, ring, j)
            copy_scales(FILL_A, inv_ag[:, 0:ER])
            for j in range(NG):
                act.wait_ge(tr_filled, GROUP_A + j + 1)
                nc.scalar.activation(AT[:, 0, GK * j:GK * (j + 1), 0:ER], chunks(ring, j), ACT.Copy).then_inc(tr_hi, 1)
            copy_scales(FILL_G, inv_ag[:, ER:HW])
            act.wait_ge(small_filled, FILL_GT + 1)
            nc.scalar.activation(AT[:, 0, :, ER:HW], small[:, 0:KC * E].rearrange("p (k e) -> p k e", k=KC),
                                 ACT.Copy).then_inc(small_hi, 1)
            bt_cols = stage[STAGE_BT].rearrange("q (p j) -> q j p", j=NJ)
            for j in range(NG):
                act.wait_ge(tr_filled, GROUP_B + j + 1)
                nc.scalar.copy(bt_cols[:, GK * j:GK * (j + 1), :], chunks(ring, j)).then_inc(bt_copied, 1)
            copy_scales(FILL_W, inv_w[:, 0:P])
            split_w_hi(0, GROUP_W)
            act.wait_ge(rows_scale, ROWS_B + 1)
            nc.scalar.activation(BT[:, 0, :], stage[STAGE_BT], ACT.Copy, scale=b_scale[:, 0:1]).then_inc(bt_hi, 1)
            copy_scales(FILL_B, inv_b[:, :])
            exp_row(0)
            for r in range(1, 4):
                if r == 2:
                    split_hwT_hi(0)
                copy_scales(FILL_W + 1 + r, inv_w[:, r * P:(r + 1) * P])
                split_w_hi(r, GROUP_W + NG * r)
            with act.Fori(1, NW // 4) as q:
                for s in range(4):
                    r = q * 4 + s
                    copy_scales(r + (FILL_W + 1), inv_w[:, bass.ds(r * P, P)])
                    split_w_hi(r, r * NG + GROUP_W)
            split_x_hi(1, 1)
            for j in range(NG):
                split_y_hi(group_y(1), tr, j)

            def period(b, par):
                exp_row(b)
                split_hwT_hi(b)
                split_x_hi(b + 1, 1 - par)
                for j in range(NG):
                    split_y_hi(group_y(b + 1), tr, j)

            with act.Fori(0, (NB - 2) // 2) as i:
                period(i * 2 + 1, 1)
                period(i * 2 + 2, 0)
            exp_row(NB - 1)
            split_hwT_hi(NB - 1)

        @block.vector
        def _(dve):
            chain = {"base": 0, "n": 0}

            def link(ins):
                chain["n"] += 1
                ins.then_inc(dve_chain, 1)
                dve.wait_ge(dve_chain, chain["base"] + chain["n"])

            def power_of_two(dst, src, clamped):
                link(nc.vector.tensor_scalar(clamped, src, TINY, None, ALU.max))
                link(nc.vector.tensor_scalar(dst.bitcast(U32), clamped.bitcast(U32), EXP_MASK, None, ALU.bitwise_and))

            def find_x_maxima(b, par, n):
                dve.wait_ge(x_in[par], 16 * (n + 1))
                nc.vector.tensor_reduce(amax[:, 0:1], X[par][:, :], AX_X, ALU.max, apply_absolute_value=True)
                dve.wait_ge(w_in, 16 * (b + 1))
                nc.vector.tensor_reduce(amax[:, 1:2], WC[:, :], AX_X, ALU.max,
                                        apply_absolute_value=True).then_inc(amax_ready, 1)

            def scale_x(b, par):
                dve.wait_ge(amax_shared, b + 1)
                power_of_two(pow2[:, :], amax_all[:, :], clamped[:, :])
                link(nc.vector.reciprocal(rpow2[:, :], pow2[:, :]))
                nc.vector.tensor_scalar(xw_scale[:, :], rpow2[:, :], TOP, None, ALU.mult).then_inc(xw_scale_ready, 1)
                link(nc.vector.scalar_tensor_tensor(out=y_inv[:, par:par + 1], in0=pow2[:, 0:1], scalar=Y_UNIT,
                                                    in1=pow2[:, 1:2], op0=ALU.mult, op1=ALU.mult))

            def split_x_lo(b, par):
                dve.wait_ge(xw_hi, b + 1)
                nc.vector.scalar_tensor_tensor(out=XP[:, 1, :], in0=X[par][:, :], scalar=xw_scale[:, 0:1],
                                               in1=XP[:, 0, :], op0=ALU.mult, op1=ALU.subtract)
                nc.vector.scalar_tensor_tensor(out=WCP[:, 1, :], in0=WC[:, :], scalar=xw_scale[:, 1:2],
                                               in1=WCP[:, 0, :], op0=ALU.mult, op1=ALU.subtract).then_inc(xw_parts, 1)

            def split_lo(hi, dst, dst_hi, src, down=1.0):
                dve.wait_ge(tr_hi, hi + 1)
                nc.vector.scalar_tensor_tensor(out=dst, in0=src, scalar=down, in1=dst_hi,
                                               op0=ALU.mult, op1=ALU.subtract).then_inc(tr_emptied, 1)

            def split_y_lo(hi, banks, j):
                ks = slice(GK * j, GK * (j + 1))
                split_lo(hi + j, Y[:, 1, ks, :], Y[:, 0, ks, :], chunks(banks, j), Y_DOWN)

            def split_w_lo(r, hi):
                for j in range(NG):
                    ks = slice(GK * j, GK * (j + 1))
                    split_lo(hi + j, WT[:, 1, ks, bass.ds(r * P, P)], WT[:, 0, ks, bass.ds(r * P, P)], chunks(ring, j))

            def scale_of_rows(rows, parity, before, scale_dst=None):
                p = rows.shape[0]
                link(nc.vector.tensor_reduce(row_max[0:p, :], rows, AX_X, ALU.max, apply_absolute_value=True))
                power_of_two(row_pow2[0:p, :], row_max[0:p, :], row_clamped[0:p, :])
                link(nc.vector.reciprocal(row_rpow2[0:p, :], row_pow2[0:p, :]))
                for used, count in before:
                    dve.wait_ge(used, count)
                if scale_dst is None:
                    nc.vector.tensor_scalar(diag[0:p, parity, 0, :], ident[0:p, :], row_rpow2[0:p, :], TOP,
                                            ALU.mult, ALU.mult)
                else:
                    nc.vector.tensor_scalar(scale_dst, row_rpow2[0:p, :], TOP, None, ALU.mult)
                nc.vector.tensor_scalar(diag[0:p, parity, 1, :], ident[0:p, :], row_pow2[0:p, :], 1.0 / TOP,
                                        ALU.mult, ALU.mult).then_inc(rows_scale, 1)

            def routing(b, par):
                dve.wait_ge(h_ready, b + 1)
                link(nc.vector.scalar_tensor_tensor(out=h[:, :], in0=h_ps[:, 0:HW], scalar=y_inv[:, par:par + 1],
                                                    in1=inv_ag[:, :], op0=ALU.mult, op1=ALU.mult))
                link(nc.vector.tensor_reduce(neg_max[:, :], h[:, ER:HW], AX_X, ALU.max, negate=True))
                nc.vector.tensor_scalar(shifted[:, :], h[:, ER:HW], neg_max[:, :], None,
                                        ALU.add).then_inc(shifted_ready, 1)
                dve.wait_ge(shifted_ready, b + 1)
                link(nc.vector.scalar_tensor_tensor(out=found[:, :], in0=shifted[:, :], scalar=0.0, in1=iota_m8[:, :],
                                                    op0=ALU.is_equal, op1=ALU.mult))
                link(nc.vector.tensor_reduce(first[:, :], found[:, :], AX_X, ALU.min))
                link(nc.vector.tensor_scalar(pick1[:, :], iota_m8[:, :], first[:, :], None, ALU.is_equal))
                link(nc.vector.scalar_tensor_tensor(out=rest[:, :], in0=pick1[:, :], scalar=-1e38, in1=shifted[:, :],
                                                    op0=ALU.mult, op1=ALU.add))
                link(nc.vector.tensor_reduce(rest_max[:, :], rest[:, :], AX_X, ALU.max))
                link(nc.vector.scalar_tensor_tensor(out=found[:, :], in0=rest[:, :], scalar=rest_max[:, :],
                                                    in1=iota_m8[:, :], op0=ALU.is_equal, op1=ALU.mult))
                link(nc.vector.tensor_reduce(first[:, :], found[:, :], AX_X, ALU.min))
                link(nc.vector.tensor_scalar(pick2[:, :], iota_m8[:, :], first[:, :], None, ALU.is_equal))
                link(nc.vector.tensor_tensor(picked[:, :], pick1[:, :], pick2[:, :], ALU.add))
                dve.wait_ge(exps_ready, b + 1)
                link(nc.vector.reciprocal(rtop[:, :], exp_sum[:, :]))
                link(nc.vector.scalar_tensor_tensor(out=top_p[:, :], in0=exps[:, :], scalar=rtop[:, :],
                                                    in1=picked[:, :], op0=ALU.mult, op1=ALU.mult))
                link(nc.vector.tensor_reduce(top_sum[:, :], top_p[:, :], AX_X, ALU.add))
                link(nc.vector.reciprocal(rtop[:, :], top_sum[:, :]))
                link(nc.vector.tensor_scalar(route[:, :], top_p[:, :], rtop[:, :], SCALING, ALU.mult, ALU.mult))
                link(nc.vector.tensor_tensor(hw[:, :, :], h[:, 0:ER].rearrange("p (e r) -> p e r", e=E),
                                             route[:, :].rearrange("p (e a) -> p e a", a=1).to_broadcast([P, E, R]),
                                             ALU.mult))
                hw_flat = hw[:, :, :].rearrange("p e r -> p (e r)")
                link(nc.vector.tensor_tensor(hw_flat, hw_flat, inv_b[:, :], ALU.mult))
                link(nc.vector.tensor_reduce(hw_max[:, :], hw_flat, AX_X, ALU.max, apply_absolute_value=True))
                power_of_two(hw_pow2[:, :], hw_max[:, :], hw_clamped[:, :])
                link(nc.vector.reciprocal(hw_rpow2[:, :], hw_pow2[:, :]))
                nc.vector.tensor_scalar(hw_inv[:, :], hw_pow2[:, :], 1.0 / TOP, None, ALU.mult)
                nc.vector.tensor_scalar(hw_flat, hw_flat, hw_rpow2[:, :], TOP, ALU.mult, ALU.mult).then_inc(hw_ready, 1)

            def split_hwT_lo(b):
                dve.wait_ge(hwT_hi, b + 1)
                nc.vector.scalar_tensor_tensor(out=hwT[:, 1, :], in0=small[:, 0:P], scalar=1.0, in1=hwT[:, 0, :],
                                               op0=ALU.mult, op1=ALU.subtract).then_inc(hwT_ready, 1)

            def finish(b, par, oc, half):
                cols = bass.ds(oc * OC, OC)
                if not (isinstance(b, int) and b == 0):
                    dve.wait_ge(finished, b * NOC + oc)
                dve.wait_ge(acc_done, b * NOC + oc + 1)
                nc.vector.scalar_tensor_tensor(out=scaled_acc[:, :], in0=acc[half][:, :], scalar=y_inv[:, par:par + 1],
                                               in1=inv_w[:, cols], op0=ALU.mult, op1=ALU.mult)
                nc.vector.scalar_tensor_tensor(out=X[par][:, cols], in0=delta[half][:, :], scalar=hw_inv[:, :],
                                               in1=X[par][:, cols], op0=ALU.mult, op1=ALU.add).then_inc(acc_read, 1)
                dve.wait_ge(acc_read, b * NOC + oc + 1)
                nc.vector.tensor_tensor(X[par][:, cols], X[par][:, cols], scaled_acc[:, :], ALU.add).then_inc(finished, 1)

            find_x_maxima(0, 0, 0)
            dve.wait_ge(consts, E + 2)
            dve.wait_ge(stage_in[STAGE_A], 16)
            scale_of_rows(stage[STAGE_A], 0, [])
            scale_x(0, 0)
            split_x_lo(0, 0)
            dve.wait_ge(stage_in[STAGE_G], 16)
            scale_of_rows(stage[STAGE_G][0:E, :], 1, [])
            for j in range(NG):
                split_y_lo(0, ring, j)
            for j in range(NG):
                ks = slice(GK * j, GK * (j + 1))
                split_lo(NG + j, AT[:, 1, ks, 0:ER], AT[:, 0, ks, 0:ER], chunks(ring, j))
            dve.wait_ge(small_hi, 1)
            nc.vector.scalar_tensor_tensor(out=AT[:, 1, :, ER:HW],
                                           in0=small[:, 0:KC * E].rearrange("p (k e) -> p k e", k=KC), scalar=1.0,
                                           in1=AT[:, 0, :, ER:HW], op0=ALU.mult,
                                           op1=ALU.subtract).then_inc(small_emptied, 1)
            dve.wait_ge(stage_in[0], 32)
            scale_of_rows(stage[0], 0, [(tr_filled, GROUP_A + NG)])
            dve.wait_ge(bt_copied, NG)
            scale_of_rows(stage[STAGE_BT], 1, [(small_filled, FILL_GT + 1)], b_scale[:, :])
            split_w_lo(0, SPLIT_W)
            dve.wait_ge(stage_in[1], 32)
            scale_of_rows(stage[1], 0, [(tr_filled, GROUP_W + NG)])
            dve.wait_ge(bt_hi, 1)
            nc.vector.scalar_tensor_tensor(out=BT[:, 1, :], in0=stage[STAGE_BT], scalar=b_scale[:, :],
                                           in1=BT[:, 0, :], op0=ALU.mult, op1=ALU.subtract).then_inc(bt_parts, 1)
            dve.wait_ge(small_emptied, FILL_B + 1)
            routing(0, 0)
            split_w_lo(1, SPLIT_W + NG)
            dve.wait_ge(stage_in[2], 32)
            scale_of_rows(stage[2], 1, [(small_filled, FILL_B + 1)])
            split_hwT_lo(0)
            dve.wait_ge(stage_in[3], 16)
            scale_of_rows(stage[3], 0, [(tr_filled, GROUP_W + NG * 2)])
            split_w_lo(2, SPLIT_W + NG * 2)

            def w_blocks(q):
                for s in range(4):
                    r = q * 4 + s
                    dve.wait_ge(stage_in[s], (q + (2 if s < 3 else 1)) * 16)
                    scale_of_rows(stage[s], (s + 1) % 2, [(tr_filled, r * NG + (GROUP_W - NG))])
                    split_w_lo(r - 1, r * NG + (SPLIT_W - NG))
                dve.wait_ge(small_emptied, q * 4 + (FILL_W + 1))
                finish(0, 0, q - 1, 0)

            start, per_block = chain["n"], 4
            with dve.Fori(1, NW // 4) as q:
                chain["base"], chain["n"] = q * (4 * per_block) + (start - 4 * per_block), 0
                w_blocks(q)
                assert chain["n"] == 4 * per_block
            chain["base"], chain["n"] = start + (NW - 4) * per_block, 0
            split_w_lo(NW - 1, SPLIT_W + NG * (NW - 1))
            dve.wait_ge(small_emptied, FILL_W + 1 + NW)
            find_x_maxima(1, 1, 0)
            scale_x(1, 1)
            split_x_lo(1, 1)
            for j in range(NG):
                split_y_lo(split_y(1), tr, j)
            finish(0, 0, NOC - 1, 1)

            def period(b, par, n):
                routing(b, par)
                split_hwT_lo(b)
                find_x_maxima(b + 1, 1 - par, n)
                scale_x(b + 1, 1 - par)
                split_x_lo(b + 1, 1 - par)
                dve.wait_ge(bias_added, b + 1)
                for oc in range(NOC - 1):
                    finish(b, par, oc, oc % 2)
                for j in range(NG):
                    split_y_lo(split_y(b + 1), tr, j)
                finish(b, par, NOC - 1, (NOC - 1) % 2)

            start, per_row = chain["base"] + chain["n"], 26
            with dve.Fori(0, (NB - 2) // 2) as i:
                for k, (b, par, n) in enumerate(((i * 2 + 1, 1, i + 1), (i * 2 + 2, 0, i + 1))):
                    chain["base"], chain["n"] = i * (2 * per_row) + (start + k * per_row), 0
                    period(b, par, n)
                    assert chain["n"] == per_row, chain["n"]
            chain["base"], chain["n"] = start + (NB - 2) * per_row, 0
            routing(NB - 1, 1)
            split_hwT_lo(NB - 1)
            dve.wait_ge(bias_added, NB)
            for oc in range(NOC):
                finish(NB - 1, 1, oc, oc % 2)

        @block.tensor
        def _(pe):
            def three(dst, lhs, rhs, start, stop):
                nc.tensor.matmul(dst, lhs[0], rhs[0], start=start, stop=False)
                nc.tensor.matmul(dst, lhs[0], rhs[1], start=False, stop=False)
                return nc.tensor.matmul(dst, lhs[1], rhs[0], start=False, stop=stop)

            def cond_group(emptied, banks, j):
                if emptied is not None:
                    pe.wait_ge(tr_emptied, emptied)
                for c in range(GK):
                    ks = slice((GK * j + c) * P, (GK * j + c + 1) * P)
                    mm = three(banks[j % len(banks)][:, c * P:(c + 1) * P], [XP[:, s, ks] for s in range(2)],
                               [WCP[:, s, :] for s in range(2)], True, True)
                mm.then_inc(tr_filled, 1)

            def lora_features(b, splits):
                for j in range(NG):
                    pe.wait_ge(tr_emptied, splits + (j + 1))
                    for k in range(GK * j, GK * (j + 1)):
                        mm = three(h_ps[:, 0:HW], [Y[:, s, k, :] for s in range(2)], [AT[:, s, k, :] for s in range(2)],
                                   k == 0, k == KC - 1)
                mm.then_inc(h_ready, 1)

            def base_step(oc, half, k):
                cols = bass.ds(oc * OC, OC)
                three(acc[half][:, :], [Y[:, s, k, :] for s in range(2)], [WT[:, s, k, cols] for s in range(2)],
                      k == 0, k == KC - 1)

            def delta_step(oc, half):
                cols = bass.ds(oc * OC, OC)
                three(delta[half][:, :], [hwT[:, s, :] for s in range(2)], [BT[:, s, cols] for s in range(2)],
                      True, True).then_inc(acc_done, 1)

            def transpose_hw(b):
                pe.wait_ge(hw_ready, b + 1)
                nc.tensor.transpose(small[:, 0:P], hw[:, :, :].rearrange("p e r -> p (e r)"),
                                    ident[:, :]).then_inc(hwT_filled, 1)

            def spread_scales(parity, ready, emptied, p=P):
                pe.wait_ge(rows_scale, ready)
                if emptied is not None:
                    pe.wait_ge(small_emptied, emptied)
                nc.tensor.matmul(small[:, 0:p], ones[0:p, :], diag[0:p, parity, 1, 0:p],
                                 start=True, stop=True).then_inc(small_filled, 1)

            def transpose_group(rows, parity, used, j):
                pe.wait_ge(*used)
                for c in range(GK):
                    dst = ring[j][:, c * P:(c + 1) * P]
                    chunk = rows[:, (GK * j + c) * P:(GK * j + c + 1) * P]
                    if parity is None:
                        mm = nc.tensor.transpose(dst, chunk, ident[:, :])
                    else:
                        mm = nc.tensor.matmul(dst, chunk, diag[:, parity, 0, :], start=True, stop=True)
                mm.then_inc(tr_filled, 1)

            pe.wait_ge(xw_parts, 1)
            for j in range(NG):
                cond_group(None, ring, j)
            pe.wait_ge(consts, E + 2)
            spread_scales(0, ROWS_A + 1, None)
            for j in range(NG):
                transpose_group(stage[STAGE_A], 0, (tr_emptied, j + 1), j)
            spread_scales(1, ROWS_G + 1, FILL_A + 1, E)
            pe.wait_ge(small_emptied, FILL_G + 1)
            for k in range(KC):
                mm = nc.tensor.matmul(small[:, k * E:(k + 1) * E], stage[STAGE_G][0:E, k * P:(k + 1) * P],
                                      diag[0:E, 1, 0, 0:E], start=True, stop=True)
            mm.then_inc(small_filled, 1)
            pe.wait_ge(b_reordered, 1)
            for j in range(NG):
                transpose_group(stage[STAGE_BJ], None, (tr_emptied, NG + j + 1), j)
            spread_scales(0, ROWS_W + 1, FILL_GT + 1)
            for j in range(NG):
                transpose_group(stage[0], 0, (bt_copied, j + 1), j)
            lora_features(0, 0)
            spread_scales(1, ROWS_B + 1, FILL_W + 1)
            for r in range(1, 4):
                if r == 2:
                    pe.wait_ge(small_emptied, FILL_W + 2 + 1)
                    transpose_hw(0)
                    pe.wait_ge(hwT_ready, 1)
                spread_scales((r + 1) % 2, ROWS_B + r + 1, FILL_W + 1 + r)
                for j in range(NG):
                    transpose_group(stage[r], (r + 1) % 2, (tr_emptied, SPLIT_W + NG * (r - 1) + j + 1), j)
            beside = {(s, j): [] for s in range(4) for j in range(NG)}
            for k, slot in zip(range(KC), [(0, 1), (0, 1), (0, 2), (0, 2), (0, 3), (0, 3), (1, 0), (1, 0), (1, 1),
                                           (1, 2), (1, 3), (2, 0), (2, 0), (2, 1), (2, 2), (2, 3)]):
                beside[slot].append(k)
            with pe.Fori(1, NW // 4) as q:
                for s in range(4):
                    spread_scales((s + 1) % 2, q * 4 + (ROWS_B + s + 1), q * 4 + (FILL_W + 1 + s))
                    for j in range(NG):
                        transpose_group(stage[s], (s + 1) % 2,
                                        (tr_emptied, q * (4 * NG) + (SPLIT_W + NG * (s - 1) + j + 1)), j)
                        for k in beside[s, j]:
                            base_step(q - 1, 0, k)
                    if s == 2:
                        delta_step(q - 1, 0)
            pe.wait_ge(tr_emptied, SPLIT_W + NG * NW)
            pe.wait_ge(small_emptied, FILL_W + 1 + NW)
            for k in range(KC):
                base_step(NOC - 1, 1, k)
                if k in (9, 11, 13, 15):
                    if k == 9:
                        pe.wait_ge(xw_parts, 2)
                    cond_group(split_y(1) + (k - 9) // 2 - 1, tr, (k - 9) // 2)
            delta_step(NOC - 1, 1)

            def period(b, last=False):
                lora_features(b, split_y(b))
                for oc in range(NOC):
                    pe.wait_ge(acc_read, b * NOC + (oc - 1))
                    for k in range(KC):
                        base_step(oc, oc % 2, k)
                        if oc == 1 and k == GK - 1:
                            pe.wait_ge(hwT_ready, b + 1)
                            delta_step(0, 0)
                        if oc == NOC - 1 and k % GK == GK - 1 and not last:
                            if k == GK - 1:
                                pe.wait_ge(xw_parts, b + 2)
                            cond_group(split_y(b + 1) + (k // GK - 1), tr, k // GK)
                    if oc == 0:
                        transpose_hw(b)
                    else:
                        delta_step(oc, oc % 2)

            with pe.Fori(1, NB - 1) as b:
                period(b)
            period(NB - 1, last=True)


_INS = ['x', 'itok_B_0_30', 'L0_cond_weights', 'L0_ffn_W_base', 'L0_ffn_b_base', 'L0_ffn_W_gate', 'L0_ffn_A',
        'L0_ffn_B']
_OUTS = [((NB, P, O), 'float32')]


def kernel(**inputs):
    import numpy as _np
    import concourse.bacc as _bacc
    from concourse import mybir as _mybir
    from concourse.bass_utils import run_bass_kernel_spmd as _run

    nc = _bacc.Bacc("TRN2", target_bir_lowering=False, num_devices=1)
    arrays, args = {}, []
    for name in _INS:
        a = _np.ascontiguousarray(inputs[name])
        arrays[f"in_{name}_dram"] = a
        args.append(nc.dram_tensor(f"in_{name}_dram", a.shape, _mybir.dt.from_np(a.dtype), kind="ExternalInput").ap())
    for i, (shape, dtype) in enumerate(_OUTS):
        dt = _mybir.dt.from_np(_np.dtype(dtype))
        args.append(nc.dram_tensor(f"out_{i}_dram", shape, dt, kind="ExternalOutput").ap())
    adaln_ffn_kernel(nc, *args)
    r = _run(nc, [arrays], core_ids=[0])
    got = tuple(r.results[0][f"out_{i}_dram"] for i in range(len(_OUTS)))
    return got[0]
```

```python
from contextlib import ExitStack

import concourse.bass as bass
from concourse import mybir

P = 128
NB = 32
T = 2048
O = 2048
KC = T // P
OC = 512
NOC = O // OC
E, R = 8, 16
ER = E * R
HW = ER + E
GK = OC // P
NG = KC // GK
NW = O // P
SCALING = 16.0 / R

TOP = 2.0 ** 14
EXP_MASK = 0x7F800000
TINY = 2.0 ** -60
Y_DOWN = 2.0 ** -22
Y_UNIT = 2.0 ** -6

ALU = mybir.AluOpType
ACT = mybir.ActivationFunctionType
F32 = mybir.dt.float32
BF16 = mybir.dt.bfloat16
F16 = mybir.dt.float16
U32 = mybir.dt.uint32
I32 = mybir.dt.int32
AX_X = mybir.AxisListType.X
RMAX = bass.bass_isa.ReduceOp.max

GROUP_W0, GROUP_A, GROUP_Y0, GROUP_B = range(0, 4 * NG, NG)
GROUP_W = 3 * NG
SPLIT_W0, SPLIT_A, SPLIT_Y0 = range(0, 3 * NG, NG)
SPLIT_W = 2 * NG
FILL_W0, FILL_G, FILL_A, FILL_GT, FILL_W1, FILL_W2, FILL_W3, FILL_B = range(8)
FILL_W = 4
ROWS_W0, ROWS_G, ROWS_A, ROWS_W1, ROWS_W2, ROWS_W3, ROWS_B = range(7)
ROWS_W = 3


def group_y(b):
    return b * NG + (GROUP_W + NG * NW - NG)


def split_y(b):
    return b * NG + (SPLIT_W + NG * NW - NG)


def adaln_ffn_kernel(nc, x, idx, w_cond, w_base, b_base, w_gate, a_lora, b_lora, out):
    with ExitStack() as ctx:
        def sb(name, shape, dt=F32):
            return ctx.enter_context(nc.sbuf_tensor(name, shape, dt))

        def bank(name):
            return ctx.enter_context(nc.psum_tensor(name, [P, OC], F32))

        def sem(name):
            return ctx.enter_context(nc.semaphore(name))

        WT = sb("WT", [P, 2, KC, O], F16)
        AT = sb("AT", [P, 2, KC, HW], F16)
        BT = sb("BT", [P, 2, O], F16)
        inv_w = sb("inv_w", [P, O], BF16)
        inv_ag = sb("inv_ag", [P, HW])
        inv_b = sb("inv_b", [P, ER])
        bias = sb("bias", [P, O])
        X = [sb("x_even", [P, T]), sb("x_odd", [P, T])]
        XP = sb("x_parts", [P, 2, T], F16)
        Y = sb("y_parts", [P, 2, KC, P], F16)
        WC = sb("w_cond", [P, P])
        WCP = sb("w_cond_parts", [P, 2, P], F16)
        spare = sb("spare", [P, T])
        scaled_acc = sb("scaled_acc", [P, OC])
        h = sb("h", [P, HW])
        hw = sb("hw", [P, E, R])
        hwT = sb("hwT", [P, 2, P], F16)
        diag = sb("diag", [P, 2, P])
        diag_inv = sb("diag_inv", [P, 2, P], BF16)
        ident = sb("ident", [P, P])
        ones = sb("ones", [P, P], BF16)
        iota_m8 = sb("iota_m8", [P, E])
        idx_sb = sb("idx", [1, NB], I32)
        amax = sb("amax", [P, 2])
        wait_taker = sb("wait_taker", [P, 2])
        amax_all = sb("amax_all", [P, 2])
        clamped = sb("clamped", [P, 2])
        pow2 = sb("pow2", [P, 2])
        rpow2 = sb("rpow2", [P, 2])
        xw_scale = sb("xw_scale", [P, 2])
        y_inv = sb("y_inv", [P, 2])
        row_sum = sb("row_sum", [P, 4])
        row_clamped = sb("row_clamped", [P, 1])
        row_pow2 = sb("row_pow2", [P, 1])
        row_rpow2 = sb("row_rpow2", [P, 1])
        row_scale = sb("row_scale", [P, 4])
        b_scale = sb("b_scale", [P, 1])
        neg_max = sb("neg_max", [P, 1])
        shifted = sb("shifted", [P, E])
        exps = sb("exps", [P, E])
        exp_sum = sb("exp_sum", [P, 1])
        found = sb("found", [P, E])
        first = sb("first", [P, 1])
        pick1 = sb("pick1", [P, E])
        rest = sb("rest", [P, E])
        rest_max = sb("rest_max", [P, 1])
        pick2 = sb("pick2", [P, E])
        picked = sb("picked", [P, E])
        top_p = sb("top_p", [P, E])
        top_sum = sb("top_sum", [P, 1])
        rtop = sb("rtop", [P, 1])
        route = sb("route", [P, E])
        hw_max = sb("hw_max", [P, 1])
        hw_clamped = sb("hw_clamped", [P, 1])
        hw_pow2 = sb("hw_pow2", [P, 1])
        hw_rpow2 = sb("hw_rpow2", [P, 1])
        hw_inv = sb("hw_inv", [P, 1])

        acc = [bank("acc0"), bank("acc1")]
        delta = [bank("delta0"), bank("delta1")]
        tr = [bank("tr0"), bank("tr1")]
        ring = tr + [acc[1], delta[1]]
        h_ps = bank("h_ps")
        hwT_ps = h_ps[:, 2 * P:3 * P]
        small = bank("small")

        xp_f32 = XP[:, :, :].rearrange("p s t -> p (s t)").bitcast(F32)
        stage = [t.rearrange("p (k n) -> p k n", k=GK) for t in (X[1][:, :], xp_f32, bias[:, :], spare[:, :])]
        b_staged = BT[:, :, :].rearrange("p s o -> p (s o)").bitcast(F32)
        b_by_column, a_staged, gate_staged, w3_staged = [WT[:, 1, GK * i:GK * (i + 1), O // 2:O].bitcast(F32)
                                                         for i in range(4)]
        gate_staged = gate_staged[0:E]
        early = [stage[0], stage[2], stage[3], w3_staged]
        b_transposed = WT[:, 0, 0:GK, O // 2:O].bitcast(F32)
        discard_a, discard_b, discard_gate = [WT[:, 0, GK * i:GK * (i + 1), O - OC:O] for i in (1, 2, 3)]
        discard_gate = discard_gate[0:E]

        idx_in = sem("idx_in")
        x_in = [sem("x_even_in"), sem("x_odd_in")]
        w_in = sem("w_in")
        stage_in = [sem(f"stage{i}_in") for i in range(4)]
        gate_in = sem("gate_in")
        a_in = sem("a_in")
        w3_in = sem("w3_in")
        b_in = sem("b_in")
        bias_in = sem("bias_in")
        out_done = [sem("out_even_done"), sem("out_odd_done")]
        consts = sem("consts")
        pool_chain = sem("pool_chain")
        amax_ready = sem("amax_ready")
        amax_shared = sem("amax_shared")
        xw_scale_ready = sem("xw_scale_ready")
        xw_hi = sem("xw_hi")
        xw_parts = sem("xw_parts")
        bias_added = sem("bias_added")
        row0_bias_added = sem("row0_bias_added")
        rows_summed = sem("rows_summed")
        rows_scale = sem("rows_scale")
        block_scaled = sem("block_scaled")
        gate_scaled = sem("gate_scaled")
        tr_filled = sem("tr_filled")
        tr_hi = sem("tr_hi")
        tr_emptied = sem("tr_emptied")
        small_filled = sem("small_filled")
        small_hi = sem("small_hi")
        small_emptied = sem("small_emptied")
        b_reordered = sem("b_reordered")
        bt_copied = sem("bt_copied")
        bt_hi = sem("bt_hi")
        bt_parts = sem("bt_parts")
        h_ready = sem("h_ready")
        shifted_ready = sem("shifted_ready")
        exps_ready = sem("exps_ready")
        hw_ready = sem("hw_ready")
        hwT_filled = sem("hwT_filled")
        hwT_hi = sem("hwT_hi")
        hwT_ready = sem("hwT_ready")
        base_done = sem("base_done")
        acc_done = sem("acc_done")
        acc_read = sem("acc_read")
        finished = sem("finished")
        dve_chain = sem("dve_chain")

        rows_w = w_base.rearrange("(n p) (k t) -> n p k t", p=P, k=GK)
        a_rows = a_lora.rearrange("e r t -> (e r) t")
        b_rows = b_lora.rearrange("e (p j) r -> p e (j r)", p=P)
        bias_row = b_base.rearrange("(a o) -> a o", a=1).to_broadcast([P, O])
        NJ = O // P

        def chunks(banks, j):
            return banks[j % len(banks)][:, :].rearrange("p (k n) -> p k n", k=GK)

        block = ctx.enter_context(nc.Block())

        @block.sync
        def _(sp):
            def load_xw(b, par):
                load_x(b, par)
                load_w(b)

            def load_x(b, par):
                sp.dma_start(X[par][:, :], x[bass.ds(b, 1)].rearrange("a p t -> p (a t)")).then_inc(x_in[par], 16)

            def load_w(b):
                row = sp.value_load(idx_sb[0:1, bass.ds(b, 1)], min_val=0, max_val=w_cond.shape[0] - 1)
                if not (isinstance(b, int) and b == 0):
                    sp.wait_ge(xw_parts, b)
                sp.dma_start(WC[:, :], w_cond[bass.ds(row, 1)].rearrange("a c d -> c (a d)")).then_inc(w_in, 16)

            def store(b, par):
                for oc in range(NOC):
                    if isinstance(b, int) and b == 0:
                        sp.wait_ge(row0_bias_added, 1 + (oc == NOC - 1))
                    else:
                        sp.wait_ge(finished, b * NOC + (oc + 1))
                    sp.dma_start(out[bass.ds(b, 1), :, oc * OC:(oc + 1) * OC].rearrange("a p t -> p (a t)"),
                                 X[par][:, oc * OC:(oc + 1) * OC]).then_inc(out_done[par], 16)

            sp.dma_start(idx_sb[:, :], idx.rearrange("(a b) -> a b", a=1)).then_inc(idx_in, 16)
            sp.dma_start(early[0], rows_w[0]).then_inc(stage_in[0], 16)
            sp.dma_start(gate_staged, w_gate.rearrange("e (k n) -> e k n", k=GK)).then_inc(gate_in, 16)
            load_x(0, 0)
            sp.wait_ge(idx_in, 16)
            load_w(0)
            sp.dma_start(a_staged, a_rows.rearrange("p (k n) -> p k n", k=GK)).then_inc(a_in, 16)
            sp.dma_start(b_staged.rearrange("p (e n) -> p e n", e=E), b_rows).then_inc(b_in, 16)
            sp.dma_start(early[1], rows_w[1]).then_inc(stage_in[2], 16)
            sp.dma_start(early[2], rows_w[2]).then_inc(stage_in[3], 16)
            sp.dma_start(early[3], rows_w[3]).then_inc(w3_in, 16)
            for r, leaves in ((4, GROUP_W0), (5, GROUP_Y0), (6, GROUP_W + NG), (7, GROUP_W + NG * 2)):
                sp.wait_ge(tr_filled, leaves + NG)
                sp.dma_start(stage[r % 4], rows_w[r]).then_inc(stage_in[r % 4], 16)
            with sp.Fori(2, NW // 4) as q:
                for s in range(4):
                    sp.wait_ge(tr_filled, q * (4 * NG) + (GROUP_W + NG * (s - 3)))
                    sp.dma_start(stage[s], rows_w[bass.ds(q * 4 + s, 1)].rearrange("a p k t -> p (a k) t")
                                 ).then_inc(stage_in[s], 16)
            sp.wait_ge(tr_filled, GROUP_W + NG * (NW - 3))
            load_xw(1, 1)
            sp.wait_ge(tr_filled, GROUP_W + NG * (NW - 1))
            sp.dma_start(bias[:, :], bias_row).then_inc(bias_in, 16)

            store(0, 0)
            sp.wait_ge(out_done[0], 16 * NOC)
            load_xw(2, 0)
            with sp.Fori(0, (NB - 4) // 2) as i:
                for b, par, n in ((i * 2 + 1, 1, i), (i * 2 + 2, 0, i + 1)):
                    store(b, par)
                    sp.wait_ge(out_done[par], (n + 1) * (16 * NOC))
                    load_xw(b + 2, par)
            store(NB - 3, 1)
            sp.wait_ge(out_done[1], 16 * NOC * (NB // 2 - 1))
            load_xw(NB - 1, 1)
            store(NB - 2, 0)
            store(NB - 1, 1)
            for par in range(2):
                sp.wait_ge(out_done[par], 16 * NOC * NB // 2)

        @block.gpsimd
        def _(pool):
            nc.gpsimd.memset(ident[:, :], 0.0).then_inc(pool_chain, 1)
            pool.wait_ge(pool_chain, 1)
            nc.gpsimd.affine_select(out=ident[:, :], in_=ident[:, :], compare_op=ALU.not_equal, fill=1.0, base=0,
                                    pattern=[[-1, P]], channel_multiplier=1).then_inc(consts, 1)
            for e in range(E):
                nc.gpsimd.memset(iota_m8[:, e:e + 1], float(e - E)).then_inc(consts, 1)
            nc.gpsimd.memset(ones[:, :], 1.0).then_inc(consts, 1)

            def share_maxima(b):
                pool.wait_ge(amax_ready, b + 1)
                nc.gpsimd.tensor_tensor(wait_taker[:, :], amax[:, :], ident[:, 0:2], ALU.mult)
                nc.gpsimd.partition_all_reduce(amax_all[:, :], amax[:, :], P, RMAX).then_inc(amax_shared, 1)

            def add_bias(par, added=bias_added, cols=slice(0, O)):
                nc.gpsimd.tensor_tensor(X[par][:, cols], X[par][:, cols], bias[:, cols], ALU.add).then_inc(added, 1)

            def scale_block(rows, n, slot):
                pool.wait_ge(rows_scale, n + 1)
                scale = row_scale[:, slot:slot + 1].rearrange("p (a b) -> p a b", a=1)
                nc.gpsimd.tensor_tensor(rows, rows, scale.to_broadcast([P, GK, OC]), ALU.mult).then_inc(block_scaled, 1)

            pool.wait_ge(consts, E + 2)
            share_maxima(0)
            pool.wait_ge(rows_scale, ROWS_G + 1)
            gate_scale = row_scale[0:E, ROWS_G:ROWS_G + 1].rearrange("p (a b) -> p a b", a=1)
            nc.gpsimd.tensor_tensor(gate_staged, gate_staged, gate_scale.to_broadcast([E, GK, OC]),
                                    ALU.mult).then_inc(gate_scaled, 1)
            pool.wait_ge(b_in, 16)
            for k in range(GK):
                part = nc.gpsimd.tensor_copy(
                    b_by_column[:, k, :].rearrange("p (j e r) -> p e j r", j=NJ // GK, e=E),
                    b_staged.rearrange("p (e j r) -> p e j r", e=E, j=NJ)[:, :, k * (NJ // GK):(k + 1) * (NJ // GK), :])
            part.then_inc(b_reordered, 1)
            for rows, n in zip(early[1:], (ROWS_W1, ROWS_W2, ROWS_W3)):
                scale_block(rows, n, n % 4)
            with pool.Fori(1, NW // 4) as q:
                for s in range(4):
                    scale_block(stage[s], q * 4 + (ROWS_W + s), (ROWS_W + s) % 4)
            share_maxima(1)
            pool.wait_ge(bias_in, 16)
            pool.wait_ge(xw_parts, 2)
            add_bias(1)
            for oc, n in ((0, NOC - 1), (NOC - 1, 1)):
                pool.wait_ge(finished, oc + n)
                add_bias(0, row0_bias_added, slice(oc * OC, (oc + n) * OC))
            with pool.Fori(0, (NB - 2) // 2) as i:
                for b, par in ((i * 2 + 2, 0), (i * 2 + 3, 1)):
                    share_maxima(b)
                    pool.wait_ge(xw_parts, b + 1)
                    add_bias(par)

        @block.scalar
        def _(act):
            def split_x_hi(b, par):
                act.wait_ge(xw_scale_ready, b + 1)
                nc.scalar.activation(XP[:, 0, :], X[par][:, :], ACT.Copy, scale=xw_scale[:, 0:1])
                nc.scalar.activation(WCP[:, 0, :], WC[:, :], ACT.Copy, scale=xw_scale[:, 1:2]).then_inc(xw_hi, 1)

            def split_y_hi(group, banks, j):
                act.wait_ge(tr_filled, group + j + 1)
                nc.scalar.activation(Y[:, 0, GK * j:GK * (j + 1), :], chunks(banks, j),
                                     ACT.Copy, scale=Y_DOWN).then_inc(tr_hi, 1)

            def sum_rows(n, rows, junk):
                slot = n % 4
                p = rows.shape[0]
                nc.scalar.activation(junk, rows, ACT.Abs,
                                     accum_out=row_sum[0:p, slot:slot + 1]).then_inc(rows_summed, 1)

            def sum_w_rows(n, r, rows, part):
                junk = WT[:, part, :, bass.ds(r * P, P)]
                sum_rows(n, rows.rearrange("p k (c n) -> p k c n", c=GK), junk.rearrange("p (k c) n -> p k c n", c=GK))

            def copy_scales(fill, dst):
                act.wait_ge(small_filled, fill + 1)
                nc.scalar.copy(dst, small[:, 0:dst.shape[1]]).then_inc(small_emptied, 1)

            def split_w_hi(r, group):
                for j in range(NG):
                    act.wait_ge(tr_filled, group + j + 1)
                    nc.scalar.activation(WT[:, 0, GK * j:GK * (j + 1), bass.ds(r * P, P)],
                                         chunks(ring, j), ACT.Copy).then_inc(tr_hi, 1)

            def exp_row(b):
                act.wait_ge(shifted_ready, b + 1)
                nc.scalar.activation(exps[:, :], shifted[:, :], ACT.Exp,
                                     accum_out=exp_sum[:, :]).then_inc(exps_ready, 1)

            def split_hwT_hi(b):
                act.wait_ge(hwT_filled, b + 1)
                nc.scalar.activation(hwT[:, 0, :], hwT_ps, ACT.Copy).then_inc(hwT_hi, 1)

            act.wait_ge(stage_in[0], 16)
            sum_w_rows(ROWS_W0, 0, early[0], 0)
            act.wait_ge(gate_in, 16)
            sum_rows(ROWS_G, gate_staged, discard_gate)
            copy_scales(FILL_W0, inv_w[:, 0:P])
            act.wait_ge(a_in, 16)
            sum_rows(ROWS_A, a_staged, discard_a)
            split_w_hi(0, GROUP_W0)
            split_x_hi(0, 0)
            copy_scales(FILL_G, inv_ag[:, ER:HW])
            for j in range(NG):
                act.wait_ge(tr_filled, GROUP_A + j + 1)
                nc.scalar.activation(AT[:, 0, GK * j:GK * (j + 1), 0:ER], chunks(ring, j), ACT.Copy).then_inc(tr_hi, 1)
            act.wait_ge(stage_in[2], 16)
            sum_w_rows(ROWS_W1, 1, early[1], 0)
            for j in range(NG):
                split_y_hi(GROUP_Y0, ring, j)
            copy_scales(FILL_A, inv_ag[:, 0:ER])
            act.wait_ge(small_filled, FILL_GT + 1)
            nc.scalar.activation(AT[:, 0, :, ER:HW], small[:, 0:KC * E].rearrange("p (k e) -> p k e", k=KC),
                                 ACT.Copy).then_inc(small_hi, 1)
            act.wait_ge(stage_in[3], 16)
            sum_w_rows(ROWS_W2, 2, early[2], 0)
            act.wait_ge(w3_in, 16)
            sum_w_rows(ROWS_W3, 3, early[3], 0)
            copy_scales(FILL_W1, inv_w[:, P:2 * P])
            act.wait_ge(bt_copied, NG)
            sum_rows(ROWS_B, b_transposed, discard_b)
            exp_row(0)
            copy_scales(FILL_W2, inv_w[:, 2 * P:3 * P])
            split_w_hi(1, GROUP_W + NG)
            copy_scales(FILL_W3, inv_w[:, 3 * P:4 * P])
            act.wait_ge(stage_in[0], 32)
            sum_w_rows(ROWS_W + 4, 4, stage[0], 1)
            split_w_hi(2, GROUP_W + 2 * NG)
            copy_scales(FILL_B, inv_b[:, :])

            def w_blocks(q, first=False):
                for s in range(first, 4):
                    r = q * 4 + s
                    act.wait_ge(stage_in[s], (q if s == 1 else q + 1) * 16)
                    sum_w_rows(ROWS_W + s, r, stage[s], 1)
                    if first and s == 2:
                        split_hwT_hi(0)
                    if not first or s >= 2:
                        copy_scales(r + (FILL_W - 2), inv_w[:, bass.ds((r - 2) * P, P)])
                    split_w_hi(r - 2, r * NG + (GROUP_W - 2 * NG))
                    if first and s == 1:
                        act.wait_ge(rows_scale, ROWS_B + 1)
                        nc.scalar.activation(BT[:, 0, :].rearrange("p (k n) -> p k n", k=GK), b_transposed, ACT.Copy,
                                             scale=b_scale[:, 0:1]).then_inc(bt_hi, 1)

            w_blocks(1, first=True)
            with act.Fori(2, NW // 4) as q:
                w_blocks(q)
            for r in (NW - 2, NW - 1):
                copy_scales(FILL_W + r, inv_w[:, r * P:(r + 1) * P])
                if r == NW - 1:
                    split_x_hi(1, 1)
                split_w_hi(r, GROUP_W + NG * r)
            for j in range(NG):
                split_y_hi(group_y(1), tr, j)

            def period(b, par):
                exp_row(b)
                split_hwT_hi(b)
                split_x_hi(b + 1, 1 - par)
                for j in range(NG):
                    split_y_hi(group_y(b + 1), tr, j)

            with act.Fori(0, (NB - 2) // 2) as i:
                period(i * 2 + 1, 1)
                period(i * 2 + 2, 0)
            exp_row(NB - 1)
            split_hwT_hi(NB - 1)

        @block.vector
        def _(dve):
            chain = {"base": 0, "n": 0}

            def link(ins):
                chain["n"] += 1
                ins.then_inc(dve_chain, 1)
                dve.wait_ge(dve_chain, chain["base"] + chain["n"])

            def power_of_two(dst, src, clamped):
                link(nc.vector.tensor_scalar(clamped, src, TINY, None, ALU.max))
                link(nc.vector.tensor_scalar(dst.bitcast(U32), clamped.bitcast(U32), EXP_MASK, None, ALU.bitwise_and))

            def find_x_maxima(b, par, n):
                dve.wait_ge(x_in[par], 16 * (n + 1))
                nc.vector.tensor_reduce(amax[:, 0:1], X[par][:, :], AX_X, ALU.max, apply_absolute_value=True)
                dve.wait_ge(w_in, 16 * (b + 1))
                nc.vector.tensor_reduce(amax[:, 1:2], WC[:, :], AX_X, ALU.max,
                                        apply_absolute_value=True).then_inc(amax_ready, 1)

            def scale_x(b, par):
                dve.wait_ge(amax_shared, b + 1)
                power_of_two(pow2[:, :], amax_all[:, :], clamped[:, :])
                link(nc.vector.reciprocal(rpow2[:, :], pow2[:, :]))
                nc.vector.tensor_scalar(xw_scale[:, :], rpow2[:, :], TOP, None, ALU.mult).then_inc(xw_scale_ready, 1)
                link(nc.vector.scalar_tensor_tensor(out=y_inv[:, par:par + 1], in0=pow2[:, 0:1], scalar=Y_UNIT,
                                                    in1=pow2[:, 1:2], op0=ALU.mult, op1=ALU.mult))

            def split_x_lo(b, par):
                dve.wait_ge(xw_hi, b + 1)
                nc.vector.scalar_tensor_tensor(out=XP[:, 1, :], in0=X[par][:, :], scalar=xw_scale[:, 0:1],
                                               in1=XP[:, 0, :], op0=ALU.mult, op1=ALU.subtract)
                nc.vector.scalar_tensor_tensor(out=WCP[:, 1, :], in0=WC[:, :], scalar=xw_scale[:, 1:2],
                                               in1=WCP[:, 0, :], op0=ALU.mult, op1=ALU.subtract).then_inc(xw_parts, 1)

            def split_lo(hi, dst, dst_hi, src, down=1.0):
                dve.wait_ge(tr_hi, hi + 1)
                nc.vector.scalar_tensor_tensor(out=dst, in0=src, scalar=down, in1=dst_hi,
                                               op0=ALU.mult, op1=ALU.subtract).then_inc(tr_emptied, 1)

            def split_y_lo(hi, banks, j):
                ks = slice(GK * j, GK * (j + 1))
                split_lo(hi + j, Y[:, 1, ks, :], Y[:, 0, ks, :], chunks(banks, j), Y_DOWN)

            def split_w_lo(r, hi, j):
                    ks = slice(GK * j, GK * (j + 1))
                    split_lo(hi + j, WT[:, 1, ks, bass.ds(r * P, P)], WT[:, 0, ks, bass.ds(r * P, P)], chunks(ring, j))

            def scale_of_rows(n, before, summed=None, p=P, scale_dst=None):
                slot, parity = n % 4, n % 2
                summed = n + 1 if summed is None else summed
                dve.wait_ge(rows_summed, summed)
                power_of_two(row_pow2[0:p, :], row_sum[0:p, slot:slot + 1], row_clamped[0:p, :])
                link(nc.vector.reciprocal(row_rpow2[0:p, :], row_pow2[0:p, :]))
                for used, count in before:
                    dve.wait_ge(used, count)
                if scale_dst is None:
                    nc.vector.tensor_scalar(diag[0:p, n // ROWS_A, :], ident[0:p, :], row_rpow2[0:p, :], TOP,
                                            ALU.mult, ALU.mult)
                else:
                    nc.vector.tensor_scalar(scale_dst, row_rpow2[0:p, :], TOP, None, ALU.mult)
                nc.vector.tensor_scalar(diag_inv[0:p, parity, :], ident[0:p, :], row_pow2[0:p, :], 1.0 / TOP,
                                        ALU.mult, ALU.mult).then_inc(rows_scale, 1)

            def scale_for_pool(n, before, count=None):
                scale_of_rows(n, before, count, scale_dst=row_scale[:, n % 4:n % 4 + 1])

            def route_tokens(b, par):
                dve.wait_ge(h_ready, b + 1)
                link(nc.vector.scalar_tensor_tensor(out=h[:, :], in0=h_ps[:, 0:HW], scalar=y_inv[:, par:par + 1],
                                                    in1=inv_ag[:, :], op0=ALU.mult, op1=ALU.mult))
                link(nc.vector.tensor_reduce(neg_max[:, :], h[:, ER:HW], AX_X, ALU.max, negate=True))
                nc.vector.tensor_scalar(shifted[:, :], h[:, ER:HW], neg_max[:, :], None,
                                        ALU.add).then_inc(shifted_ready, 1)
                dve.wait_ge(shifted_ready, b + 1)
                link(nc.vector.scalar_tensor_tensor(out=found[:, :], in0=shifted[:, :], scalar=0.0, in1=iota_m8[:, :],
                                                    op0=ALU.is_equal, op1=ALU.mult))
                link(nc.vector.tensor_reduce(first[:, :], found[:, :], AX_X, ALU.min))
                link(nc.vector.tensor_scalar(pick1[:, :], iota_m8[:, :], first[:, :], None, ALU.is_equal))
                link(nc.vector.scalar_tensor_tensor(out=rest[:, :], in0=pick1[:, :], scalar=-1e38, in1=shifted[:, :],
                                                    op0=ALU.mult, op1=ALU.add))
                link(nc.vector.tensor_reduce(rest_max[:, :], rest[:, :], AX_X, ALU.max))
                link(nc.vector.scalar_tensor_tensor(out=found[:, :], in0=rest[:, :], scalar=rest_max[:, :],
                                                    in1=iota_m8[:, :], op0=ALU.is_equal, op1=ALU.mult))
                link(nc.vector.tensor_reduce(first[:, :], found[:, :], AX_X, ALU.min))
                link(nc.vector.tensor_scalar(pick2[:, :], iota_m8[:, :], first[:, :], None, ALU.is_equal))
                link(nc.vector.tensor_tensor(picked[:, :], pick1[:, :], pick2[:, :], ALU.add))
                dve.wait_ge(exps_ready, b + 1)
                link(nc.vector.reciprocal(rtop[:, :], exp_sum[:, :]))
                link(nc.vector.scalar_tensor_tensor(out=top_p[:, :], in0=exps[:, :], scalar=rtop[:, :],
                                                    in1=picked[:, :], op0=ALU.mult, op1=ALU.mult))
                link(nc.vector.tensor_reduce(top_sum[:, :], top_p[:, :], AX_X, ALU.add))
                link(nc.vector.reciprocal(rtop[:, :], top_sum[:, :]))
                link(nc.vector.tensor_scalar(route[:, :], top_p[:, :], rtop[:, :], SCALING, ALU.mult, ALU.mult))

            def weigh_features(b):
                link(nc.vector.tensor_tensor(hw[:, :, :], h[:, 0:ER].rearrange("p (e r) -> p e r", e=E),
                                             route[:, :].rearrange("p (e a) -> p e a", a=1).to_broadcast([P, E, R]),
                                             ALU.mult))
                hw_flat = hw[:, :, :].rearrange("p e r -> p (e r)")
                link(nc.vector.tensor_tensor(hw_flat, hw_flat, inv_b[:, :], ALU.mult))
                link(nc.vector.tensor_reduce(hw_max[:, :], hw_flat, AX_X, ALU.max, apply_absolute_value=True))
                power_of_two(hw_pow2[:, :], hw_max[:, :], hw_clamped[:, :])
                link(nc.vector.reciprocal(hw_rpow2[:, :], hw_pow2[:, :]))
                nc.vector.tensor_scalar(hw_inv[:, :], hw_pow2[:, :], 1.0 / TOP, None, ALU.mult)
                nc.vector.tensor_scalar(hw_flat, hw_flat, hw_rpow2[:, :], TOP, ALU.mult, ALU.mult).then_inc(hw_ready, 1)

            def split_hwT_lo(b):
                dve.wait_ge(hwT_hi, b + 1)
                nc.vector.scalar_tensor_tensor(out=hwT[:, 1, :], in0=hwT_ps, scalar=1.0, in1=hwT[:, 0, :],
                                               op0=ALU.mult, op1=ALU.subtract).then_inc(hwT_ready, 1)

            def finish_base(b, par, oc, half, done=acc_done):
                if not (isinstance(oc, int) and isinstance(b, int) and b == oc == 0):
                    dve.wait_ge(finished, b * NOC + oc)
                dve.wait_ge(done, b * NOC + oc + 1)
                nc.vector.scalar_tensor_tensor(out=scaled_acc[:, :], in0=acc[half][:, :], scalar=y_inv[:, par:par + 1],
                                               in1=inv_w[:, bass.ds(oc * OC, OC)], op0=ALU.mult, op1=ALU.mult)

            def finish_delta(b, par, oc, half):
                cols = bass.ds(oc * OC, OC)
                dve.wait_ge(acc_done, b * NOC + oc + 1)
                nc.vector.scalar_tensor_tensor(out=X[par][:, cols], in0=delta[half][:, :], scalar=hw_inv[:, :],
                                               in1=X[par][:, cols], op0=ALU.mult, op1=ALU.add).then_inc(acc_read, 1)
                dve.wait_ge(acc_read, b * NOC + oc + 1)
                nc.vector.tensor_tensor(X[par][:, cols], X[par][:, cols], scaled_acc[:, :],
                                        ALU.add).then_inc(finished, 1)

            def finish(b, par, oc, half):
                finish_base(b, par, oc, half)
                finish_delta(b, par, oc, half)

            dve.wait_ge(consts, E + 2)
            scale_of_rows(ROWS_W0, [])
            find_x_maxima(0, 0, 0)
            scale_of_rows(ROWS_G, [], p=E, scale_dst=row_scale[0:E, ROWS_G:ROWS_G + 1])
            scale_x(0, 0)
            scale_of_rows(ROWS_A, [(small_filled, FILL_W0 + 1)])
            for j in range(NG):
                split_w_lo(0, SPLIT_W0, j)
            split_x_lo(0, 0)
            for j in range(NG):
                ks = slice(GK * j, GK * (j + 1))
                split_lo(SPLIT_A + j, AT[:, 1, ks, 0:ER], AT[:, 0, ks, 0:ER], chunks(ring, j))
            scale_for_pool(ROWS_W1, [(small_filled, FILL_G + 1)])
            for j in range(NG):
                split_y_lo(SPLIT_Y0, ring, j)
            dve.wait_ge(small_hi, 1)
            nc.vector.scalar_tensor_tensor(out=AT[:, 1, :, ER:HW],
                                           in0=small[:, 0:KC * E].rearrange("p (k e) -> p k e", k=KC), scalar=1.0,
                                           in1=AT[:, 0, :, ER:HW], op0=ALU.mult,
                                           op1=ALU.subtract).then_inc(small_emptied, 1)
            bt_cols = b_transposed.rearrange("q k (p j) -> q j k p", j=NJ)
            for j in range(NG):
                dve.wait_ge(tr_filled, GROUP_B + j + 1)
                nc.vector.tensor_copy(bt_cols[:, GK * j:GK * (j + 1), :, :],
                                      chunks(ring, j).rearrange("q c (k p) -> q c k p", k=GK)).then_inc(bt_copied, 1)
            scale_for_pool(ROWS_W2, [(small_filled, FILL_A + 1)])
            scale_for_pool(ROWS_W3, [(small_filled, FILL_W1 + 1)])
            dve.wait_ge(small_emptied, FILL_A + 1)
            route_tokens(0, 0)
            scale_of_rows(ROWS_B, [(small_filled, FILL_W2 + 1)], scale_dst=b_scale[:, :])
            for j in range(NG):
                split_w_lo(1, SPLIT_W + NG, j)
            scale_for_pool(ROWS_W + 4, [(small_filled, FILL_W3 + 1)])
            for j in range(NG):
                split_w_lo(2, SPLIT_W + NG * 2, j)
            dve.wait_ge(small_emptied, FILL_B + 1)
            weigh_features(0)

            def w_blocks(q, first=False):
                for s in range(first, 4):
                    r = q * 4 + s
                    scale_for_pool(ROWS_W + s, [(small_filled, r + (FILL_W - 1))], r + (ROWS_W + 1))
                    for j in range(NG):
                        split_w_lo(r - 2, r * NG + (SPLIT_W - 2 * NG), j)
                        if s == 2 and j == 1:
                            dve.wait_ge(small_emptied, q * 4 + FILL_W)
                            finish_base(0, 0, q - 1, 0, base_done)
                    if s == 1 and not first:
                        finish_delta(0, 0, q - 2, 0)
                    if s == 1 and first:
                        dve.wait_ge(bt_hi, 1)
                        nc.vector.scalar_tensor_tensor(out=BT[:, 1, :].rearrange("p (k n) -> p k n", k=GK),
                                                       in0=b_transposed, scalar=b_scale[:, :],
                                                       in1=BT[:, 0, :].rearrange("p (k n) -> p k n", k=GK),
                                                       op0=ALU.mult, op1=ALU.subtract).then_inc(bt_parts, 1)
                    if s == 2 and first:
                        split_hwT_lo(0)

            w_blocks(1, first=True)
            start, per_block = chain["n"], 3
            with dve.Fori(2, NW // 4) as q:
                chain["base"], chain["n"] = q * (4 * per_block) + (start - 8 * per_block), 0
                w_blocks(q)
                assert chain["n"] == 4 * per_block, chain["n"]
            chain["base"], chain["n"] = start + (NW - 8) * per_block, 0
            find_x_maxima(1, 1, 0)
            for j in range(NG):
                split_w_lo(NW - 2, SPLIT_W + NG * (NW - 2), j)
                if j == 1:
                    scale_x(1, 1)
            split_x_lo(1, 1)
            for j in range(NG):
                split_w_lo(NW - 1, SPLIT_W + NG * (NW - 1), j)
            finish_delta(0, 0, NOC - 2, 0)
            dve.wait_ge(small_emptied, FILL_W + NW)
            finish_base(0, 0, NOC - 1, 0, base_done)
            for j in range(NG):
                split_y_lo(split_y(1), tr, j)
            finish_delta(0, 0, NOC - 1, 1)

            def period(b, par, n):
                route_tokens(b, par)
                weigh_features(b)
                split_hwT_lo(b)
                find_x_maxima(b + 1, 1 - par, n)
                scale_x(b + 1, 1 - par)
                split_x_lo(b + 1, 1 - par)
                dve.wait_ge(bias_added, b)
                for oc in range(NOC - 1):
                    finish(b, par, oc, oc % 2)
                for j in range(NG):
                    split_y_lo(split_y(b + 1), tr, j)
                finish(b, par, NOC - 1, (NOC - 1) % 2)

            start, per_row = chain["base"] + chain["n"], 26
            with dve.Fori(0, (NB - 2) // 2) as i:
                for k, (b, par, n) in enumerate(((i * 2 + 1, 1, i + 1), (i * 2 + 2, 0, i + 1))):
                    chain["base"], chain["n"] = i * (2 * per_row) + (start + k * per_row), 0
                    period(b, par, n)
                    assert chain["n"] == per_row, chain["n"]
            chain["base"], chain["n"] = start + (NB - 2) * per_row, 0
            route_tokens(NB - 1, 1)
            weigh_features(NB - 1)
            split_hwT_lo(NB - 1)
            dve.wait_ge(bias_added, NB - 1)
            for oc in range(NOC):
                finish(NB - 1, 1, oc, oc % 2)

        @block.tensor
        def _(pe):
            def three(dst, lhs, rhs, start, stop):
                nc.tensor.matmul(dst, lhs[0], rhs[0], start=start, stop=False)
                nc.tensor.matmul(dst, lhs[0], rhs[1], start=False, stop=False)
                return nc.tensor.matmul(dst, lhs[1], rhs[0], start=False, stop=stop)

            def cond_group(emptied, banks, j):
                if emptied is not None:
                    pe.wait_ge(tr_emptied, emptied)
                for c in range(GK):
                    ks = slice((GK * j + c) * P, (GK * j + c + 1) * P)
                    mm = three(banks[j % len(banks)][:, c * P:(c + 1) * P], [XP[:, s, ks] for s in range(2)],
                               [WCP[:, s, :] for s in range(2)], True, True)
                mm.then_inc(tr_filled, 1)

            def lora_features(b, splits):
                for j in range(NG):
                    pe.wait_ge(tr_emptied, splits + (j + 1))
                    for k in range(GK * j, GK * (j + 1)):
                        mm = three(h_ps[:, 0:HW], [Y[:, s, k, :] for s in range(2)], [AT[:, s, k, :] for s in range(2)],
                                   k == 0, k == KC - 1)
                mm.then_inc(h_ready, 1)

            def base_step(oc, half, k):
                cols = bass.ds(oc * OC, OC)
                three(acc[half][:, :], [Y[:, s, k, :] for s in range(2)], [WT[:, s, k, cols] for s in range(2)],
                      k == 0, k == KC - 1)

            def delta_step(oc, half):
                cols = bass.ds(oc * OC, OC)
                three(delta[half][:, :], [hwT[:, s, :] for s in range(2)], [BT[:, s, cols] for s in range(2)],
                      True, True).then_inc(acc_done, 1)

            def transpose_hw(b):
                pe.wait_ge(hw_ready, b + 1)
                nc.tensor.transpose(hwT_ps, hw[:, :, :].rearrange("p e r -> p (e r)"),
                                    ident[:, :]).then_inc(hwT_filled, 1)

            def spread_scales(parity, ready, emptied, p=P):
                pe.wait_ge(rows_scale, ready)
                if emptied is not None:
                    pe.wait_ge(small_emptied, emptied)
                nc.tensor.matmul(small[:, 0:p], ones[0:p, :], diag_inv[0:p, parity, 0:p],
                                 start=True, stop=True).then_inc(small_filled, 1)

            def transpose_group(rows, scales, used, j):
                pe.wait_ge(*used)
                for c in range(GK):
                    dst, chunk = ring[j][:, c * P:(c + 1) * P], rows[:, j, c * P:(c + 1) * P]
                    if scales is None:
                        mm = nc.tensor.transpose(dst, chunk, ident[:, :])
                    else:
                        mm = nc.tensor.matmul(dst, chunk, diag[:, scales, :], start=True, stop=True)
                mm.then_inc(tr_filled, 1)

            pe.wait_ge(consts, E + 2)
            spread_scales(ROWS_W0 % 2, ROWS_W0 + 1, None)
            for j in range(NG):
                transpose_group(early[0], 0, (rows_scale, ROWS_W0 + 1), j)
            spread_scales(ROWS_G % 2, ROWS_G + 1, FILL_W0 + 1, E)
            pe.wait_ge(rows_scale, ROWS_A + 1)
            for j in range(NG):
                transpose_group(a_staged, 1, (tr_emptied, SPLIT_W0 + j + 1), j)
            pe.wait_ge(xw_parts, 1)
            for j in range(NG):
                cond_group(SPLIT_A + j + 1, ring, j)
            spread_scales(ROWS_A % 2, ROWS_A + 1, FILL_G + 1)
            pe.wait_ge(small_emptied, FILL_A + 1)
            pe.wait_ge(gate_scaled, 1)
            for k in range(KC):
                mm = nc.tensor.transpose(small[:, k * E:(k + 1) * E],
                                         gate_staged[:, k // GK, k % GK * P:(k % GK + 1) * P], ident[0:E, 0:E])
            mm.then_inc(small_filled, 1)
            pe.wait_ge(b_reordered, 1)
            for j in range(NG):
                transpose_group(b_by_column, None, (tr_emptied, SPLIT_Y0 + j + 1), j)
            spread_scales(ROWS_W1 % 2, ROWS_W1 + 1, FILL_GT + 1)
            lora_features(0, SPLIT_Y0)
            spread_scales(ROWS_W2 % 2, ROWS_W2 + 1, FILL_W1 + 1)

            def w_block(r, rows, column, done=None):
                pe.wait_ge(block_scaled, r)
                for j in range(NG):
                    used = (bt_copied, j + 1) if isinstance(r, int) and r == 1 else \
                        (tr_emptied, r * NG + (SPLIT_W - NG + j + 1))
                    transpose_group(rows, None, used, j)
                    if j > 1:
                        block_steps(r - 1, column, j - 2)
                for j in (NG - 2, NG - 1):
                    product = block_steps(r - 1, column, j)
                if done is not None:
                    product.then_inc(done, 1)

            def block_steps(r, column, j):
                for k in range(GK * j, GK * (j + 1)):
                    product = three(acc[0][:, column * P:(column + 1) * P], [Y[:, s, k, :] for s in range(2)],
                                    [WT[:, s, k, bass.ds(r * P, P)] for s in range(2)], k == 0, k == KC - 1)
                return product

            w_block(1, early[1], 0)
            spread_scales(ROWS_W3 % 2, ROWS_W3 + 1, FILL_W2 + 1)
            w_block(2, early[2], 1)
            spread_scales(ROWS_B % 2, ROWS_B + 1, FILL_W3 + 1)
            w_block(3, early[3], 2)

            def w_blocks(q, first=False):
                for s in range(4):
                    r = q * 4 + s
                    spread_scales((ROWS_W + s) % 2, r + (ROWS_W + 1), r + FILL_W)
                    w_block(r, stage[s], (s - 1) % GK, base_done if s == 0 else None)
                    if first and s == 0:
                        transpose_hw(0)
                if first:
                    pe.wait_ge(hwT_ready, 1)
                    pe.wait_ge(bt_parts, 1)
                delta_step(q - 1, 0)

            w_blocks(1, first=True)
            with pe.Fori(2, NW // 4) as q:
                w_blocks(q)
            for j in range(NG):
                pe.wait_ge(tr_emptied, SPLIT_W + NG * (NW - 1) + j + 1)
                product = block_steps(NW - 1, GK - 1, j)
                if j == NG - 1:
                    product.then_inc(base_done, 1)
                    delta_step(NOC - 1, 1)
                if j == 1:
                    pe.wait_ge(xw_parts, 2)
                if j > 0:
                    cond_group(split_y(1) + j - 2, tr, j - 1)
            cond_group(split_y(1) + NG - 2, tr, NG - 1)

            def period(b, last=False):
                lora_features(b, split_y(b))
                for oc in range(NOC):
                    pe.wait_ge(acc_read, b * NOC + (oc - 1))
                    for k in range(KC):
                        base_step(oc, oc % 2, k)
                        if oc == 1 and k == GK - 1:
                            pe.wait_ge(hwT_ready, b + 1)
                            delta_step(0, 0)
                        if oc == NOC - 1 and k % GK == GK - 1 and not last:
                            if k == GK - 1:
                                pe.wait_ge(xw_parts, b + 2)
                            cond_group(split_y(b + 1) + (k // GK - 1), tr, k // GK)
                    if oc == 0:
                        transpose_hw(b)
                    else:
                        delta_step(oc, oc % 2)

            with pe.Fori(1, NB - 1) as b:
                period(b)
            period(NB - 1, last=True)


_INS = ['x', 'itok_B_0_30', 'L0_cond_weights', 'L0_ffn_W_base', 'L0_ffn_b_base', 'L0_ffn_W_gate', 'L0_ffn_A',
        'L0_ffn_B']
_OUTS = [((NB, P, O), 'float32')]


def kernel(**inputs):
    import numpy as _np
    import concourse.bacc as _bacc
    from concourse import mybir as _mybir
    from concourse.bass_utils import run_bass_kernel_spmd as _run

    nc = _bacc.Bacc("TRN2", target_bir_lowering=False, num_devices=1)
    arrays, args = {}, []
    for name in _INS:
        a = _np.ascontiguousarray(inputs[name])
        arrays[f"in_{name}_dram"] = a
        args.append(nc.dram_tensor(f"in_{name}_dram", a.shape, _mybir.dt.from_np(a.dtype), kind="ExternalInput").ap())
    for i, (shape, dtype) in enumerate(_OUTS):
        dt = _mybir.dt.from_np(_np.dtype(dtype))
        args.append(nc.dram_tensor(f"out_{i}_dram", shape, dt, kind="ExternalOutput").ap())
    adaln_ffn_kernel(nc, *args)
    r = _run(nc, [arrays], core_ids=[0])
    got = tuple(r.results[0][f"out_{i}_dram"] for i in range(len(_OUTS)))
    return got[0]
```
